# Optimizing a Trainium2 kernel written in Bass

```python
import numpy as np
import jax
import jax.numpy as jnp

def _softmax(x, axis=-1):
    return jax.nn.softmax(x, axis=axis)

def _gelu(x):
    return jax.nn.gelu(x, approximate=True)

def _silu(x):
    return jax.nn.silu(x)

def _sigmoid(x):
    return jax.nn.sigmoid(x)

def _layernorm(x, axis=-1, eps=1e-05):
    m = jnp.mean(x, axis=axis, keepdims=True)
    v = jnp.var(x, axis=axis, keepdims=True)
    return (x - m) / jnp.sqrt(v + eps)

def _scatter_add(tgt, idx, src, axis=0):
    return tgt.at[idx].add(src)

def _segment_sum(src, seg, n):
    return jax.ops.segment_sum(src, seg, n)
kernel_name = 'mk_prb_d1_jaxref_r8_9972d9'

def setup_inputs(seed: int=0):
    np.random.seed(seed)
    _w = jnp.asarray

    def _L0_attn_setup():
        import jax, jax.numpy as jnp
        import numpy as np
        N_EMBD = 128
        N_HEAD = 16
        MASK_FILL = -10000.0
        key = jax.random.key(seed)
        ks = jax.random.split(key, 9)
        s = 1.0 / np.sqrt(N_EMBD)
        d = {'x': jax.random.normal(ks[0], (4, 256, N_EMBD), dtype=jnp.float32)}
        for i, name in enumerate(['k', 'q', 'v', 'p']):
            d[f'W{name}'] = jax.random.uniform(ks[1 + 2 * i], (N_EMBD, N_EMBD), minval=-s, maxval=s, dtype=jnp.float32)
            d[f'b{name}'] = jax.random.uniform(ks[2 + 2 * i], (N_EMBD,), minval=-s, maxval=s, dtype=jnp.float32)
        return d
    _L0_attn_in = _L0_attn_setup()

    def _L0_ffn_setup():
        import jax, jax.numpy as jnp
        import numpy as np
        DIM = 128
        DEPTH = 6
        HEADS = 16
        DIM_HEAD = 64
        WINDOW = 32
        INNER = HEADS * DIM_HEAD
        DIM_INNER = int(DIM * 4 * 2 / 3)
        QK_SCALE = 8.0

        def shift_tokens(t):
            a, s = jnp.split(t, 2, -1)
            s = jnp.pad(s, ((0, 0), (1, 0), (0, 0)))[:, :-1]
            return jnp.concatenate([a, s], -1)

        def l2norm(t):
            return t / jnp.maximum(jnp.linalg.norm(t, axis=-1, keepdims=True), 1e-12)

        def rotate_half(x):
            x1, x2 = jnp.split(x, 2, -1)
            return jnp.concatenate([-x2, x1], -1)

        def rotary_tables(n):
            half = jnp.arange(0, DIM_HEAD, 2, dtype=jnp.float32)
            inv_freq = 1.0 / 10000.0 ** (half / DIM_HEAD)
            t = jnp.arange(n, dtype=jnp.float32)
            freqs = t[:, None] * inv_freq[None, :]
            freqs = jnp.concatenate([freqs, freqs], -1)
            base_scale = (half + 0.4 * DIM_HEAD) / (1.4 * DIM_HEAD)
            power = (t - n // 2) / (WINDOW // 2)
            scale = base_scale[None, :] ** power[:, None]
            scale = jnp.concatenate([scale, scale], -1)
            return (freqs, scale)

        def local_attention(q, k, v):
            b, h, n, d = q.shape
            w = WINDOW
            nw = n // w
            bq = q.reshape(b, h, nw, w, d)
            bk = k.reshape(b, h, nw, w, d)
            bv = v.reshape(b, h, nw, w, d)

            def look(t):
                p = jnp.pad(t, ((0, 0), (0, 0), (1, 0), (0, 0), (0, 0)))
                return jnp.concatenate([p[:, :, :nw], p[:, :, 1:]], axis=3)
            bk2, bv2 = (look(bk), look(bv))
            seq = jnp.arange(n).reshape(nw, w)
            seq_p = jnp.pad(seq, ((1, 0), (0, 0)), constant_values=-1)
            jt = jnp.concatenate([seq_p[:nw], seq_p[1:]], axis=1)
            it = seq[:, :, None]
            jb = jt[:, None, :]
            mask = (it < jb) | (it > jb + w) | (jb == -1)
            sim = jnp.einsum('bhwie,bhwje->bhwij', bq, bk2) * QK_SCALE
            sim = jnp.where(mask, -jnp.finfo(sim.dtype).max, sim)
            attn = jax.nn.softmax(sim, -1)
            out = jnp.einsum('bhwij,bhwje->bhwie', attn, bv2)
            return out.reshape(b, h, n, d)

        def attn_layer(x, Wqkv, qs, ksc, Wo):
            b, n, _ = x.shape
            qkv = x @ Wqkv
            q, k, v = jnp.split(qkv, 3, -1)
            sh = lambda t: t.reshape(b, n, HEADS, DIM_HEAD).transpose(0, 2, 1, 3)
            q, k, v = (sh(q), sh(k), sh(v))
            q = l2norm(q) * qs
            k = l2norm(k) * ksc
            freqs, scale = rotary_tables(n)
            cos, sin = (jnp.cos(freqs), jnp.sin(freqs))
            q = q * cos * scale + rotate_half(q) * sin * scale
            inv = 1.0 / scale
            k = k * cos * inv + rotate_half(k) * sin * inv
            out = local_attention(q, k, v)
            out = out.transpose(0, 2, 1, 3).reshape(b, n, INNER)
            return out @ Wo

        def ffn_layer(x, g, bln, W1, b1, W2, b2):
            mu = x.mean(-1, keepdims=True)
            var = ((x - mu) ** 2).mean(-1, keepdims=True)
            xn = (x - mu) / jnp.sqrt(var + 1e-05) * g + bln
            hg = xn @ W1 + b1
            a, gate = jnp.split(hg, 2, -1)
            return a * jax.nn.gelu(gate, approximate=False) @ W2 + b2
        key = jax.random.key(seed)
        ks = jax.random.split(key, 8)
        B, N = (2, 256)
        init = lambda k, shape: jax.random.normal(k, shape, jnp.float32) * 0.02
        return {'x': jax.random.normal(ks[0], (B, N, DIM), jnp.float32), 'Wqkv': init(ks[1], (DEPTH, DIM, 3 * INNER)), 'q_scale': jnp.ones((DEPTH, DIM_HEAD), jnp.float32), 'k_scale': jnp.ones((DEPTH, DIM_HEAD), jnp.float32), 'Wo': init(ks[2], (DEPTH, INNER, DIM)), 'ln_g': jnp.ones((DEPTH, DIM), jnp.float32), 'ln_b': jnp.zeros((DEPTH, DIM), jnp.float32), 'W1': init(ks[3], (DEPTH, DIM, 2 * DIM_INNER)), 'b1': jnp.zeros((DEPTH, 2 * DIM_INNER), jnp.float32), 'W2': init(ks[4], (DEPTH, DIM_INNER, DIM)), 'b2': jnp.zeros((DEPTH, DIM), jnp.float32)}
    _L0_ffn_in = _L0_ffn_setup()
    _d = {'L0_attn_x': _L0_attn_in['x'], 'L0_attn_Wk': _L0_attn_in['Wk'], 'L0_attn_bk': _L0_attn_in['bk'], 'L0_attn_Wq': _L0_attn_in['Wq'], 'L0_attn_bq': _L0_attn_in['bq'], 'L0_attn_Wv': _L0_attn_in['Wv'], 'L0_attn_bv': _L0_attn_in['bv'], 'L0_attn_Wp': _L0_attn_in['Wp'], 'L0_attn_bp': _L0_attn_in['bp'], 'L0_ffn_Wqkv': _L0_ffn_in['Wqkv'], 'L0_ffn_q_scale': _L0_ffn_in['q_scale'], 'L0_ffn_k_scale': _L0_ffn_in['k_scale'], 'L0_ffn_Wo': _L0_ffn_in['Wo'], 'L0_ffn_ln_g': _L0_ffn_in['ln_g'], 'L0_ffn_ln_b': _L0_ffn_in['ln_b'], 'L0_ffn_W1': _L0_ffn_in['W1'], 'L0_ffn_b1': _L0_ffn_in['b1'], 'L0_ffn_W2': _L0_ffn_in['W2'], 'L0_ffn_b2': _L0_ffn_in['b2']}
    _x0 = _d['L0_attn_x']
    _d['L0_attn_x'] = jax.random.normal(jax.random.fold_in(jax.random.key(seed), 1), (8, 512, 128), dtype=_x0.dtype)
    del _x0
    return _d

def reference(L0_attn_x, L0_attn_Wk, L0_attn_bk, L0_attn_Wq, L0_attn_bq, L0_attn_Wv, L0_attn_bv, L0_attn_Wp, L0_attn_bp, L0_ffn_Wqkv, L0_ffn_q_scale, L0_ffn_k_scale, L0_ffn_Wo, L0_ffn_ln_g, L0_ffn_ln_b, L0_ffn_W1, L0_ffn_b1, L0_ffn_W2, L0_ffn_b2):

    def _L0_attn_ref(x, Wk, bk, Wq, bq, Wv, bv, Wp, bp):
        import jax, jax.numpy as jnp
        import numpy as np
        N_EMBD = 128
        N_HEAD = 16
        MASK_FILL = -10000.0
        B, T, C = x.shape
        H, D = (N_HEAD, C // N_HEAD)

        def split_heads(y):
            return y.reshape(B, T, H, D).transpose(0, 2, 1, 3)
        k = split_heads(x @ Wk + bk)
        q = split_heads(x @ Wq + bq)
        v = split_heads(x @ Wv + bv)
        att = jnp.einsum('bhtd,bhsd->bhts', q, k) / jnp.sqrt(jnp.float32(D))
        causal = jnp.tril(jnp.ones((T, T), dtype=bool))
        att = jnp.where(causal[None, None], att, MASK_FILL)
        att = jax.nn.softmax(att, axis=-1)
        y = jnp.einsum('bhts,bhsd->bhtd', att, v)
        y = y.transpose(0, 2, 1, 3).reshape(B, T, C)
        return y @ Wp + bp

    def _L0_ffn_ref(x, Wqkv, q_scale, k_scale, Wo, ln_g, ln_b, W1, b1, W2, b2):
        import jax, jax.numpy as jnp
        import numpy as np
        DIM = 128
        DEPTH = 6
        HEADS = 16
        DIM_HEAD = 64
        WINDOW = 32
        INNER = HEADS * DIM_HEAD
        DIM_INNER = int(DIM * 4 * 2 / 3)
        QK_SCALE = 8.0

        def shift_tokens(t):
            a, s = jnp.split(t, 2, -1)
            s = jnp.pad(s, ((0, 0), (1, 0), (0, 0)))[:, :-1]
            return jnp.concatenate([a, s], -1)

        def l2norm(t):
            return t / jnp.maximum(jnp.linalg.norm(t, axis=-1, keepdims=True), 1e-12)

        def rotate_half(x):
            x1, x2 = jnp.split(x, 2, -1)
            return jnp.concatenate([-x2, x1], -1)

        def rotary_tables(n):
            half = jnp.arange(0, DIM_HEAD, 2, dtype=jnp.float32)
            inv_freq = 1.0 / 10000.0 ** (half / DIM_HEAD)
            t = jnp.arange(n, dtype=jnp.float32)
            freqs = t[:, None] * inv_freq[None, :]
            freqs = jnp.concatenate([freqs, freqs], -1)
            base_scale = (half + 0.4 * DIM_HEAD) / (1.4 * DIM_HEAD)
            power = (t - n // 2) / (WINDOW // 2)
            scale = base_scale[None, :] ** power[:, None]
            scale = jnp.concatenate([scale, scale], -1)
            return (freqs, scale)

        def local_attention(q, k, v):
            b, h, n, d = q.shape
            w = WINDOW
            nw = n // w
            bq = q.reshape(b, h, nw, w, d)
            bk = k.reshape(b, h, nw, w, d)
            bv = v.reshape(b, h, nw, w, d)

            def look(t):
                p = jnp.pad(t, ((0, 0), (0, 0), (1, 0), (0, 0), (0, 0)))
                return jnp.concatenate([p[:, :, :nw], p[:, :, 1:]], axis=3)
            bk2, bv2 = (look(bk), look(bv))
            seq = jnp.arange(n).reshape(nw, w)
            seq_p = jnp.pad(seq, ((1, 0), (0, 0)), constant_values=-1)
            jt = jnp.concatenate([seq_p[:nw], seq_p[1:]], axis=1)
            it = seq[:, :, None]
            jb = jt[:, None, :]
            mask = (it < jb) | (it > jb + w) | (jb == -1)
            sim = jnp.einsum('bhwie,bhwje->bhwij', bq, bk2) * QK_SCALE
            sim = jnp.where(mask, -jnp.finfo(sim.dtype).max, sim)
            attn = jax.nn.softmax(sim, -1)
            out = jnp.einsum('bhwij,bhwje->bhwie', attn, bv2)
            return out.reshape(b, h, n, d)

        def attn_layer(x, Wqkv, qs, ksc, Wo):
            b, n, _ = x.shape
            qkv = x @ Wqkv
            q, k, v = jnp.split(qkv, 3, -1)
            sh = lambda t: t.reshape(b, n, HEADS, DIM_HEAD).transpose(0, 2, 1, 3)
            q, k, v = (sh(q), sh(k), sh(v))
            q = l2norm(q) * qs
            k = l2norm(k) * ksc
            freqs, scale = rotary_tables(n)
            cos, sin = (jnp.cos(freqs), jnp.sin(freqs))
            q = q * cos * scale + rotate_half(q) * sin * scale
            inv = 1.0 / scale
            k = k * cos * inv + rotate_half(k) * sin * inv
            out = local_attention(q, k, v)
            out = out.transpose(0, 2, 1, 3).reshape(b, n, INNER)
            return out @ Wo

        def ffn_layer(x, g, bln, W1, b1, W2, b2):
            mu = x.mean(-1, keepdims=True)
            var = ((x - mu) ** 2).mean(-1, keepdims=True)
            xn = (x - mu) / jnp.sqrt(var + 1e-05) * g + bln
            hg = xn @ W1 + b1
            a, gate = jnp.split(hg, 2, -1)
            return a * jax.nn.gelu(gate, approximate=False) @ W2 + b2
        for i in range(DEPTH):
            x = attn_layer(shift_tokens(x), Wqkv[i], q_scale[i], k_scale[i], Wo[i]) + x
            x = ffn_layer(shift_tokens(x), ln_g[i], ln_b[i], W1[i], b1[i], W2[i], b2[i]) + x
        return x
    x = L0_attn_x
    xn = _layernorm(x, axis=-1)
    x = x + _L0_attn_ref(xn, L0_attn_Wk, L0_attn_bk, L0_attn_Wq, L0_attn_bq, L0_attn_Wv, L0_attn_bv, L0_attn_Wp, L0_attn_bp) + _L0_ffn_ref(xn, L0_ffn_Wqkv, L0_ffn_q_scale, L0_ffn_k_scale, L0_ffn_Wo, L0_ffn_ln_g, L0_ffn_ln_b, L0_ffn_W1, L0_ffn_b1, L0_ffn_W2, L0_ffn_b2)
    return x

_drawn_inputs = setup_inputs


def setup_inputs(seed=0):
    import zlib

    import numpy as np

    out = dict(_drawn_inputs(seed))
    spreads = {'L0_ffn_q_scale': (1.0, 0.6),
     'L0_ffn_k_scale': (1.0, 0.6),
     'L0_ffn_ln_g': (1.0, 0.6),
     'L0_ffn_ln_b': (0.0, 0.8),
     'L0_ffn_b1': (0.0, 0.8),
     'L0_ffn_b2': (0.0, 0.1)}
    factors = {'L0_attn_Wk': 7.517,
     'L0_attn_bk': 64.0,
     'L0_attn_Wq': 7.731,
     'L0_attn_bq': 8.0,
     'L0_attn_Wv': 2.875,
     'L0_attn_bv': 10.266,
     'L0_ffn_W1': 3.64,
     'L0_ffn_W2': 3.575,
     'L0_attn_bp': 6.475}
    for name, (base, spread) in spreads.items():
        noise = np.random.default_rng([zlib.crc32(name.encode()), seed]).standard_normal(out[name].shape)
        drawn = base * np.exp(spread * noise) if base else spread * noise
        out[name] = jnp.asarray(drawn.astype(out[name].dtype))
    for name, factor in factors.items():
        out[name] = (out[name] * factor).astype(out[name].dtype)
    return out
```

```python
from contextlib import ExitStack

import concourse.bass as bass
from concourse import mybir

F32 = mybir.dt.float32
BF16 = mybir.dt.bfloat16
I32 = mybir.dt.int32
ALU = mybir.AluOpType
ACT = mybir.ActivationFunctionType
AX = mybir.AxisListType

P = 128
B, N, C = 8, 512, 128
ROWS = B * N
RT = ROWS // P
NT = N // P
DEPTH = 6
HEADS, DH = 16, 64
PAIRS = HEADS // 2
INNER = HEADS * DH
W = 32
GQ = 2 * W
GK = GQ + W
NG = N // GQ
FI = 341
FB = [(0, 128), (128, 128), (256, 85)]
UNITS = B * PAIRS
RSQRT_SEED = 0x5F3759DF
LN_EPS = 1e-5


def newton_rsqrt(dve, link, y, x, t):
    link(dve.tensor_scalar(y.bitcast(I32), x.bitcast(I32), -0.5, float(RSQRT_SEED), ALU.mult, ALU.add))
    for _ in range(3):
        link(dve.scalar_tensor_tensor(out=t, in0=y, scalar=-0.5, in1=y, op0=ALU.mult, op1=ALU.mult))
        link(dve.tensor_tensor(t, t, x, ALU.mult))
        link(dve.scalar_tensor_tensor(out=y, in0=t, scalar=1.5, in1=y, op0=ALU.add, op1=ALU.mult))


def layernorm_to_state(nc, x, ident_d, x_rows, state, ident, psum):
    with ExitStack() as ctx:
        def sb(name, shape, dt=F32):
            return ctx.enter_context(nc.sbuf_tensor(name, shape, dt))

        def sem(name):
            return ctx.enter_context(nc.semaphore(name))

        centred = sb("ln_centred", [P, RT, C])
        squares = sb("ln_squares", [P, RT, C])
        total = sb("ln_total", [P, RT])
        mean = sb("ln_mean", [P, RT])
        var = sb("ln_var", [P, RT])
        rstd = sb("ln_rstd", [P, RT])
        tmp = sb("ln_tmp", [P, RT])
        x_loaded, ident_loaded = sem("x_loaded"), sem("ident_loaded")
        ln_step, ln_ready, turned, evacuated = sem("ln_step"), sem("ln_ready"), sem("ln_turned"), sem("ln_evacuated")
        x_v = x.rearrange("b (t p) c -> p (b t) c", p=P)
        block = ctx.enter_context(nc.Block())

        @block.sync
        def _(sp):
            sp.dma_start(ident[:], ident_d).then_inc(ident_loaded, 16)
            sp.dma_start(x_rows[:], x_v).then_inc(x_loaded, 16)

        @block.vector
        def _(dve):
            steps = [0]

            def link(ins):
                steps[0] += 1
                ins.then_inc(ln_step, 1)
                dve.wait_ge(ln_step, steps[0])

            dve.wait_ge(x_loaded, 16)
            link(dve.tensor_reduce(total[:], x_rows[:], AX.X, ALU.add))
            link(dve.tensor_scalar(mean[:], total[:], 1.0 / C, None, ALU.mult))
            link(dve.tensor_tensor(centred[:], x_rows[:], mean[:].unsqueeze(2).broadcast_to([P, RT, C]), ALU.subtract))
            link(dve.tensor_tensor(squares[:], centred[:], centred[:], ALU.mult))
            link(dve.tensor_reduce(total[:], squares[:], AX.X, ALU.add))
            link(dve.tensor_scalar(var[:], total[:], 1.0 / C, LN_EPS, ALU.mult, ALU.add))
            newton_rsqrt(dve, link, rstd[:], var[:], tmp[:])
            dve.tensor_tensor(centred[:], centred[:], rstd[:].unsqueeze(2).broadcast_to([P, RT, C]),
                              ALU.mult).then_inc(ln_ready, 1)

        @block.tensor
        def _(pe):
            pe.wait_ge(ident_loaded, 16)
            pe.wait_ge(ln_ready, 1)
            for g in range(RT // 4):
                for j in range(4):
                    last = pe.transpose(psum[:, g % 8, j * P:(j + 1) * P], centred[:, 4 * g + j, :], ident[:])
                last.then_inc(turned, 1)

        @block.scalar
        def _(act):
            for g in range(RT // 4):
                act.wait_ge(turned, g + 1)
                last = act.copy(state[:, g * 512:(g + 1) * 512], psum[:, g % 8, :])
            last.then_inc(evacuated, 1)


def causal_attention(nc, wk, bk, wq, bq, wv, bv, wp, bp, causal_masks, x_rows, state, ident, psum):
    H, D = 16, 8
    PARTS = 3
    KR = D * PARTS * PARTS
    SKEW = 3
    GH = 4
    VW = 32
    LANES = 8
    SCALE = float(D) ** -0.5
    MAX_BANKS, EXP_BANKS, VALUES, MISC_A, MISC_B = (0, 1), (2, 3, 4), 5, 6, 7
    ROW_USES = [[(3, 0)], [(2, 0), (0, 384)], [(1, 0)]]
    KEY_USES = [[(0, 0)], [(1, 0), (3, 384)], [(2, 0)]]
    KEY_COL = {0: 0, 1: 512, 3: 896, 2: 1024}
    with ExitStack() as ctx:
        def sb(name, shape, dt=F32):
            return ctx.enter_context(nc.sbuf_tensor(name, shape, dt))

        def sem(name):
            return ctx.enter_context(nc.semaphore(name))

        w = sb("att_w", [P, 4, P])
        bias = sb("att_bias", [P, 2])
        bias_rows = sb("att_bias_rows", [P, 2, P])
        masks = sb("att_masks", [P, 2, P], BF16)
        identb = sb("att_identb", [P, P], BF16)
        xs = sb("att_x", [P, N])
        f32s = sb("att_qk", [P, 2, N])
        rest = sb("att_rest", [P, 2, N])
        parts = sb("att_parts", [P, 2, PARTS, N], BF16)
        v_rows = sb("att_v", [P, 2, NT, P])
        vx = sb("att_vx", [P, NT, H, VW])
        stacked = sb("att_stacked", [P, 2, 2, H, N], BF16)
        top = sb("att_top", [P, NT, H])
        low = sb("att_low", [P, NT, H])
        neg = sb("att_neg", [P, NT, 2, H], BF16)
        neg_t = sb("att_neg_t", [2 * H, N], BF16)
        probs_t = sb("att_probs_t", [P, LANES, NT * (NT + 1) // 2 * P])
        o_ext = sb("att_o_ext", [P, N])
        rden = sb("att_rden", [P, NT, GH])
        o_rows = sb("att_o_rows", [P, NT, P])
        o_t = sb("att_o_t", [P, N])
        scratch = nc.dram_tensor("att_scratch", (2, 2, P, PARTS * PARTS, N), BF16, kind="Internal").ap()
        scratch_neg = nc.dram_tensor("att_scratch_neg", (2, 2 * H, N), BF16, kind="Internal").ap()

        loaded, consts, ones_set = sem("a_loaded"), sem("a_consts"), sem("a_ones")
        x_copied, q_raw, k_raw, v_raw = sem("a_x_copied"), sem("a_q_raw"), sem("a_k_raw"), sem("a_v_raw")
        q_biased, k_biased, v_ready, vx_ready = sem("a_q_biased"), sem("a_k_biased"), sem("a_v_ready"), sem("a_vx_ready")
        split_step, split = sem("a_split_step"), [sem("a_q_split"), sem("a_k_split")]
        stored = [sem("a_q_stored"), sem("a_k_stored")]
        stacked_in = [[sem("a_low_in_even"), sem("a_low_in_odd")], [sem("a_high_in_even"), sem("a_high_in_odd")]]
        row_scores, row_max = sem("a_row_scores"), sem("a_row_max")
        neg_step, neg_ready, neg_turned, neg_t_ready = (sem("a_neg_step"), sem("a_neg_ready"), sem("a_neg_turned"),
                                                        sem("a_neg_t_ready"))
        neg_stored, neg_in = sem("a_neg_stored"), sem("a_neg_in")
        key_scores, key_exp, valued = sem("a_key_scores"), sem("a_key_exp"), sem("a_valued")
        o_copied, o_turned, o_step, o_ready = sem("a_o_copied"), sem("a_o_turned"), sem("a_o_step"), sem("a_o_ready")
        o_back, o_t_ready, out_made, out_added = sem("a_o_back"), sem("a_o_t_ready"), sem("a_out_made"), sem("a_out_added")
        sw = state[:].rearrange("p (b n) -> p b n", b=B)

        def iterations(eng, iteration):
            iteration(0, 0, True, False, False)
            iteration(1, 1, True, True, False)
            with eng.Fori(1, B // 2) as m:
                for par in range(2):
                    i = eng.alloc_register(f"att_iteration_{par}")
                    eng.reg_mov(i, 2 * m + par)
                    iteration(eng.snap(i), par, True, True, True)
            iteration(B, 0, False, True, True)
            iteration(B + 1, 1, False, False, True)

        def groups_at(slot):
            g = (slot - 8) // GH if slot >= 8 and slot % GH == 0 else None
            t = (slot - 9) // GH if slot >= 9 and slot % GH == 1 else None
            return g, t
        SLOTS = H + SKEW + 3

        block = ctx.enter_context(nc.Block())

        @block.sync
        def _(sp):
            def row(v):
                return v.rearrange("(o c) -> o c", o=1).broadcast_to([P, P])
            for dst, src in ((w[:, 0], wq), (w[:, 1], wk), (w[:, 2], wv), (w[:, 3], wp),
                             (bias[:, 0:1], bq.rearrange("(c o) -> c o", o=1)), (bias[:, 1:2], bk.rearrange("(c o) -> c o", o=1)),
                             (bias_rows[:, 0], row(bv)), (bias_rows[:, 1], row(bp)),
                             (rest[:, 0, 0:2 * P], causal_masks.rearrange("p a k -> p (a k)"))):
                sp.dma_start(dst, src).then_inc(loaded, 16)
            sp.wait_ge(ones_set, 1)

            def iteration(i, par, prep, pass1, pass2):
                if prep:
                    for j in range(2):
                        sp.wait_ge(split[j], i + 1)
                        dst = scratch[par, j].rearrange("p (a b) n -> p a b n", a=PARTS)
                        for a in range(PARTS):
                            src = parts[:, 0, a:a + 1].broadcast_to([P, PARTS, N]) if j == 0 else parts[:, 1]
                            sp.dma_start(dst[:, a], src).then_inc(stored[j], 16)
                    for j in range(2):
                        sp.wait_ge(stored[j], 48 * i + 48)
                    for c in range(2):
                        if pass2:
                            sp.wait_ge(key_scores, 48 * (i - 2) + 24 * (c + 1))
                        for j in range(2):
                            sp.dma_start(stacked[0:KR, par, j, 8 * c:8 * c + 8, :],
                                         scratch[par, j].rearrange("(h d) a n -> (d a) h n", d=D)[:, 8 * c:8 * c + 8]) \
                                .then_inc(stacked_in[c][par], 16)
                if pass1:
                    sp.wait_ge(neg_t_ready, i)
                    sp.dma_start(scratch_neg[1 - par], neg_t[:]).then_inc(neg_stored, 16)
                    sp.wait_ge(neg_stored, 16 * i)
                    sp.dma_start(stacked[KR:KR + 2, 1 - par, 0], scratch_neg[1 - par].rearrange("(a h) n -> a h n", a=2)) \
                        .then_inc(neg_in, 16)

            iterations(sp, iteration)

        @block.tensor
        def _(pe):
            pe.wait_ge(loaded, 144)
            pe.wait_ge(consts, 5)

            def iteration(i, par, prep, pass1, pass2):
                n1, n2 = i - 1, i - 2

                def prepare_qk():
                    pe.wait_ge(x_copied, i + 1)
                    pe.wait_ge(v_ready, i)
                    if pass2:
                        pe.wait_ge(o_t_ready, i - 1)
                        pe.wait_ge(out_added, i - 1)
                    pe.wait_ge(k_biased, i)
                    if pass1:
                        pe.wait_ge(neg_t_ready, i - 1)
                    pe.matmul(psum[:, MISC_A, :], w[:, 0], xs[:], start=True, stop=True).then_inc(q_raw, 1)
                    pe.matmul(psum[:, MISC_B, :], w[:, 1], xs[:], start=True, stop=True).then_inc(k_raw, 1)

                def prepare_v():
                    pe.wait_ge(q_biased, i + 1)
                    for t in range(NT):
                        last = pe.matmul(psum[:, MISC_A, t * P:(t + 1) * P], xs[:, t * P:(t + 1) * P], w[:, 2],
                                         start=True, stop=True)
                    last.then_inc(v_raw, 1)

                def scores(n, h, p_, uses, banks, free, done, rows, mask, spans):
                    for j, use in enumerate(uses):
                        free(j)
                        bank = banks(j)
                        for t, c0 in use:
                            (lhs, l0), (rhs, r0), width, diag = spans(t)
                            for a, b, on_mask in ((0, diag, False), (diag, diag + P, True), (diag + P, width, False)):
                                if a >= b:
                                    continue
                                dst = psum[:, bank, c0 + a:c0 + b]
                                if on_mask:
                                    pe.matmul(dst, identb[:], mask, start=True, stop=True)
                                last = pe.matmul(dst, stacked[0:rows, p_, lhs, h, l0:l0 + P],
                                                 stacked[0:rows, p_, rhs, h, r0 + a:r0 + b],
                                                 start=not on_mask, stop=True, skip_group_check=on_mask)
                        last.then_inc(done, 1)

                def pass_one(h):
                    if h % 8 == 0:
                        pe.wait_ge(stacked_in[h // 8][1 - par], 16 * (n1 - (1 - par)) + 32)

                    def free(j):
                        if 3 * h + j >= 2:
                            pe.wait_ge(row_max, 48 * n1 + 3 * h + j - 1)
                        else:
                            pe.wait_ge(row_max, 48 * n1)
                    scores(n1, h, 1 - par, ROW_USES, lambda j: MAX_BANKS[(3 * h + j) % 2], free, row_scores, KR,
                           masks[:, 0], lambda t: ((0, t * P), (1, 0), (t + 1) * P, t * P))

                def pass_two(h):
                    if h == 0:
                        pe.wait_ge(neg_in, 16 * n2 + 16)
                    scores(n2, h, par, KEY_USES, lambda j: EXP_BANKS[j],
                           lambda j: pe.wait_ge(key_exp, 48 * n2 + 3 * h + j - 1) if 3 * h + j > 2 else
                           pe.wait_ge(key_exp, 48 * n2 + 1), key_scores, KR + 2,
                           masks[:, 1], lambda t: ((1, t * P), (0, t * P), N - t * P, 0))

                def values(g):
                    pe.wait_ge(vx_ready, n2 + 1)
                    pe.wait_ge(key_exp, 48 * n2 + 12 * g + 13)
                    pe.wait_ge(o_copied, 4 * n2 + g + 1)
                    for t in range(NT):
                        for j in range(GH):
                            h = GH * g + j
                            last = pe.matmul(psum[VW * j:VW * j + VW, VALUES, t * P:N], vx[:, t, h, :],
                                             probs_t[:, h % LANES, KEY_COL[t]:KEY_COL[t] + N - t * P],
                                             start=t == 0, stop=t == NT - 1, skip_group_check=True)
                    last.then_inc(valued, 1)

                def turn_output(g):
                    pe.wait_ge(o_copied, 4 * n2 + g + 2)
                    if g == 0 and prep:
                        pe.wait_ge(v_ready, i + 1)
                    if g == 1 and prep:
                        pe.wait_ge(k_biased, i + 1)
                    if g == 3 and pass1:
                        pe.wait_ge(neg_t_ready, i)
                    if g >= 2:
                        pe.wait_ge(o_ready, 4 * n2 + g)
                    for t in range(NT):
                        last = pe.transpose(psum[:, MISC_A + g % 2, t * P:(t + 1) * P], o_ext[:, t * P:(t + 1) * P],
                                            ident[:])
                    last.then_inc(o_turned, 1)

                def turn_maxima():
                    pe.wait_ge(neg_ready, n1 + 1)
                    if pass2:
                        pe.wait_ge(o_ready, 4 * n2 + 3)
                    if prep:
                        pe.wait_ge(k_biased, i + 1)
                    turned = psum[0:2 * H, MISC_B, 0:N // 2].bitcast(BF16)
                    for t in range(NT):
                        last = pe.transpose(turned[:, t * P:(t + 1) * P], neg[:, t].rearrange("p a h -> p (a h)"),
                                            identb[:])
                    last.then_inc(neg_turned, 1)

                for s in range(SLOTS):
                    if s == 0 and prep:
                        prepare_qk()
                    if pass1 and s < H:
                        pass_one(s)
                    if s == 1 and prep:
                        prepare_v()
                    if pass2 and SKEW <= s < H + SKEW:
                        pass_two(s - SKEW)
                    g, t = groups_at(s)
                    if pass1 and s == H + 1:
                        turn_maxima()
                    if pass2 and g is not None:
                        values(g)
                    if pass2 and t is not None:
                        turn_output(t)
                if pass2:
                    pe.wait_ge(o_ready, 4 * n2 + 5)
                    for t in range(NT):
                        last = pe.transpose(psum[:, MISC_A, t * P:(t + 1) * P], o_rows[:, t, :], ident[:])
                    last.then_inc(o_back, 1)
                    pe.wait_ge(o_t_ready, n2 + 2)
                    for t in range(NT):
                        last = pe.matmul(psum[:, MISC_B, t * P:(t + 1) * P], o_t[:, t * P:(t + 1) * P], w[:, 3],
                                         start=True, stop=True)
                    last.then_inc(out_made, 1)

            iterations(pe, iteration)

        @block.scalar
        def _(act):
            act.wait_ge(loaded, 144)

            def iteration(i, par, prep, pass1, pass2):
                n2 = i - 2
                if prep:
                    for j, (raw, done) in enumerate(((q_raw, q_biased), (k_raw, k_biased))):
                        act.wait_ge(raw, i + 1)
                        act.wait_ge(split[j], i)
                        act.activation(f32s[:, j], psum[:, MISC_A + j, :], ACT.Identity,
                                       bias=bias[:, j:j + 1]).then_inc(done, 1)
                for s in range(SLOTS):
                    if pass2 and SKEW <= s < H + SKEW:
                        h = s - SKEW
                        if h % GH == 0:
                            act.wait_ge(valued, 4 * n2 + h // GH + 1)
                        for j, c0, c in ((0, 0, 512), (1, 512, 512), (2, 1024, 256)):
                            act.wait_ge(key_scores, 48 * n2 + 3 * h + j + 1)
                            act.activation(probs_t[:, h % LANES, c0:c0 + c], psum[:, EXP_BANKS[j], 0:c], ACT.Exp,
                                           scale=SCALE).then_inc(key_exp, 1)
                    g, t = groups_at(s)
                    if pass1 and s == H + 1:
                        act.wait_ge(neg_turned, i)
                        if i is not None:
                            act.wait_ge(neg_stored, 16 * (i - 1))
                        act.copy(neg_t[:], psum[0:2 * H, MISC_B, 0:N // 2].bitcast(BF16)).then_inc(neg_t_ready, 1)
                    if pass2 and g is not None:
                        act.wait_ge(valued, 4 * n2 + g + 1 + 2)
                        act.wait_ge(o_turned, 4 * n2 + g + 1)
                        act.copy(o_ext[:], psum[:, VALUES, :]).then_inc(o_copied, 1)
                if pass2:
                    act.wait_ge(o_back, n2 + 2)
                    act.wait_ge(out_made, n2 + 1)
                    act.copy(o_t[:], psum[:, MISC_A, :]).then_inc(o_t_ready, 1)

            iterations(act, iteration)

        @block.vector
        def _(dve):
            dve.memset(stacked[64:96, :, 1], 1.0).then_inc(ones_set, 1)
            dve.memset(vx[:], 0.0).then_inc(consts, 1)
            dve.wait_ge(consts, 1)
            dve.memset(vx[:, :, :, D:D + 1], 1.0).then_inc(consts, 1)
            for counted in (o_turned, out_made, o_back, o_ready, key_exp, o_copied, o_t_ready, out_added):
                dve.sem_inc(counted, 1)
            dve.sem_inc(valued, 2)
            dve.wait_ge(loaded, 144)
            dve.tensor_tensor(x_rows[:], x_rows[:], bias_rows[:, 1].unsqueeze(1).broadcast_to([P, RT, P]),
                              ALU.add).then_inc(consts, 1)
            dve.tensor_copy(masks[:].rearrange("p a k -> p (a k)"), rest[:, 0, 0:2 * P]).then_inc(consts, 1)
            dve.tensor_copy(identb[:], ident[:]).then_inc(consts, 1)
            dve.wait_ge(consts, 5)

            def iteration(i, par, prep, pass1, pass2):
                n1, n2 = i - 1, i - 2

                def split_parts(j):
                    dve.wait_ge((q_biased, k_biased)[j], i + 1)
                    dve.wait_ge(stored[j], 48 * i)
                    steps = [8 * i + 4 * j]

                    def link(ins):
                        steps[0] = steps[0] + 1
                        ins.then_inc(split_step, 1)
                        dve.wait_ge(split_step, steps[0])

                    link(dve.tensor_copy(parts[:, j, 0], f32s[:, j]))
                    link(dve.tensor_tensor(rest[:, j], f32s[:, j], parts[:, j, 0], ALU.subtract))
                    link(dve.tensor_copy(parts[:, j, 1], rest[:, j]))
                    link(dve.tensor_tensor(rest[:, j], rest[:, j], parts[:, j, 1], ALU.subtract))
                    dve.tensor_copy(parts[:, j, 2], rest[:, j]).then_inc(split[j], 1)

                def row_maxima(h):
                    for j, use in enumerate(ROW_USES):
                        dve.wait_ge(row_scores, 48 * n1 + 3 * h + j + 1)
                        if h == 0 and j == 0:
                            dve.wait_ge(neg_ready, n1)
                        for t, c0 in use:
                            last = dve.tensor_reduce(top[:, t, h:h + 1],
                                                     psum[:, MAX_BANKS[(3 * h + j) % 2], c0:c0 + (t + 1) * P], AX.X, ALU.max)
                        last.then_inc(row_max, 1)

                if pass2:
                    dve.wait_ge(valued, 4 * n2 + 2)
                    dve.tensor_copy(vx[:, :, :, 0:D], v_rows[:, par].rearrange("p t (h d) -> p t h d", d=D)) \
                        .then_inc(vx_ready, 1)
                if prep:
                    dve.wait_ge(v_raw, i)
                    dve.tensor_copy(xs[:].unsqueeze(1), sw[:, bass.ds(i, 1), :]).then_inc(x_copied, 1)
                for s in range(SLOTS):
                    if pass1 and s < H:
                        row_maxima(s)
                    if prep and s in (0, 1):
                        split_parts(s)
                    if prep and s == 1:
                        dve.wait_ge(v_raw, i + 1)
                        if pass2:
                            dve.wait_ge(vx_ready, n2 + 1)
                        dve.tensor_tensor(v_rows[:, par], psum[:, MISC_A, :].rearrange("p (t c) -> p t c", t=NT),
                                          bias_rows[:, 0].unsqueeze(1).broadcast_to([P, NT, P]), ALU.add) \
                            .then_inc(v_ready, 1)
                    if pass1 and s == H - 1:
                        dve.wait_ge(row_max, 48 * n1 + 48)
                        dve.wait_ge(neg_turned, n1)
                        dve.tensor_scalar(neg[:, :, 0], top[:], -1.0, None, ALU.mult).then_inc(neg_step, 1)
                        dve.wait_ge(neg_step, 2 * n1 + 1)
                        dve.tensor_tensor(low[:], top[:], neg[:, :, 0], ALU.add).then_inc(neg_step, 1)
                        dve.wait_ge(neg_step, 2 * n1 + 2)
                        dve.tensor_scalar(neg[:, :, 1], low[:], -1.0, None, ALU.mult).then_inc(neg_ready, 1)
                    g, t = groups_at(s)
                    if pass2 and t is not None:
                        dve.wait_ge(o_turned, 4 * n2 + t + 2)
                        dve.wait_ge(o_ready, 4 * n2 + t + 1)
                        src = psum[:, MISC_A + t % 2, :].rearrange("p (t h c) -> p t h c", t=NT, h=GH)
                        dve.reciprocal(rden[:], src[:, :, :, D]).then_inc(o_step, 1)
                        dve.wait_ge(o_step, 4 * n2 + t + 1)
                        if t == 0:
                            dve.wait_ge(o_back, n2 + 1)
                        dve.tensor_tensor(o_rows[:, :, GH * D * t:GH * D * (t + 1)].rearrange("p t (h d) -> p t h d", d=D),
                                          src[:, :, :, 0:D], rden[:].unsqueeze(3).broadcast_to([P, NT, GH, D]), ALU.mult) \
                            .then_inc(o_ready, 1)
                if pass2:
                    dve.wait_ge(out_made, n2 + 2)
                    xb = x_rows[:, bass.ds(NT * n2, NT), :]
                    dve.tensor_tensor(xb, psum[:, MISC_B, :].rearrange("p (t c) -> p t c", t=NT), xb, ALU.add) \
                        .then_inc(out_added, 1)

            iterations(dve, iteration)


def layers(nc, w_qkv, q_scale, k_scale, w_o, w_1, w_2, columns, rotary, window_mask, state, ident, psum):
    T_LAG, S_LAG, V_LAG, O_LAG = 1, 2, 3, 4
    with ExitStack() as ctx:
        def sb(name, shape, dt=F32):
            return ctx.enter_context(nc.sbuf_tensor(name, shape, dt))

        def sem(name):
            return ctx.enter_context(nc.semaphore(name))

        wqkv = sb("wqkv", [P, 3, PAIRS, P])
        wo = sb("wo", [P, PAIRS, P])
        w1 = sb("w1", [P, 2 * FI])
        w2 = sb("w2", [P, len(FB), P])
        cols = sb("cols", [P, 9])
        base = sb("rotary_base", [P, 4, N])
        table = sb("rotary_table", [P, 4, N])
        scales = sb("scales", [P, 2, DEPTH, DH])
        mask = sb("mask", [P, NT * GK], BF16)
        identb = sb("identb", [P, P], BF16)
        mean_w = sb("mean_w", [P, P])
        eps_col = sb("eps_col", [P, 1])
        xs = sb("xs", [P, N])
        sq_q = sb("sq_q", [P, 2, N])
        sq_k = sb("sq_k", [P, 2, N])
        products_of = sb("rotary_products", [P, 4, 2, N])
        cos_q, sin_q, cos_k, sin_k = (products_of[:, i] for i in range(4))
        q_rot, k_rot = sb("q_rot", [P, 2, N]), sb("k_rot", [P, 2, N])
        sums = sb("norm_sums", [P, 2, 16])
        rnorm = sb("rnorm", [P, 4, 16])
        ntmp = sb("norm_tmp", [P, 16])
        q_t = sb("q_t", [P, 2, N])
        k_t = sb("k_t", [P, 2, 2, W + N])
        v_rows = sb("v_rows", [P, 2, NT, P])
        v_grp = sb("v_grp", [GK, 4, NG, P])
        top = sb("score_max", [P, 2, 2, NT])
        nbias = sb("score_nbias", [P, 2, 2, NT])
        den = sb("den", [P, 2, 2, NT])
        rden = sb("rden", [P, 2, 2, NT])
        probs = sb("probs", [P, 2, 2, NT * GK])
        probs_t = sb("probs_t", [GK, 2, N])
        att_t = sb("att_t", [P, N])
        xf = sb("xf", [P, 2, N])
        xc = sb("xc", [P, 2, N])
        xsq = sb("xsq", [P, 2, N])
        std = sb("std", [P, 2, N])
        normed = sb("normed", [P, ROWS])
        gate = sb("gate", [P, 2, len(FB), N])
        hid = products_of[:, 0:3].rearrange("p j h n -> p h j n")

        RAW_Q, RAW_K, V_ATT, Q_T, S_A, S_B, TURN, OUT = range(8)

        consts_loaded, consts_set = sem("consts_loaded"), sem("consts_set")
        att_w_loaded, ffn_w_loaded, tables_ready = sem("att_w_loaded"), sem("ffn_w_loaded"), sem("tables_ready")
        shifted = sem("shifted")
        q_raw, k_raw, v_raw = sem("q_raw"), sem("k_raw"), sem("v_raw")
        q_squared, k_squared, v_copied = sem("q_squared"), sem("k_squared"), sem("v_copied")
        q_products, k_products = sem("q_products"), sem("k_products")
        q_summed, k_summed = sem("q_summed"), sem("k_summed")
        norm_step, k_step = sem("norm_step"), sem("k_step")
        q_rotated, k_rotated = sem("q_rotated"), sem("k_rotated")
        q_turned, k_turned, q_t_ready, k_t_ready = sem("q_turned"), sem("k_turned"), sem("q_t_ready"), sem("k_t_ready")
        v_grouped = [sem(f"v_grouped{i}") for i in range(4)]
        scored, maxed, biased = sem("scored"), sem("maxed"), sem("biased")
        exped = [sem("exped_a"), sem("exped_b")]
        inverted = [sem("inverted_a"), sem("inverted_b")]
        weighed = [sem("weighed_a"), sem("weighed_b")]
        p_turned = [sem("p_turned_a"), sem("p_turned_b")]
        p_t_ready = [sem("p_t_ready_a"), sem("p_t_ready_b")]
        attended, att_t_ready, projected, att_added = sem("attended"), sem("att_t_ready"), sem("projected"), sem("att_added")
        f_shifted, mean_ready, centred, squared, var_ready = (sem("f_shifted"), sem("mean_ready"), sem("f_centred"),
                                                              sem("f_squared"), sem("var_ready"))
        std_ready, f_step, ln_done = sem("std_ready"), sem("f_step"), sem("ln_done")
        gate_raw, hid_raw, gelu_done, hid_ready = sem("gate_raw"), sem("hid_raw"), sem("gelu_done"), sem("hid_ready")
        ffn_raw, ffn_added = sem("ffn_raw"), sem("ffn_added")
        sw = state[:].rearrange("p (b n) -> p b n", b=B)
        nw = normed[:].rearrange("p (b n) -> p b n", b=B)

        def pipeline(eng, iteration, feed_forward):
            with eng.Fori(0, DEPTH) as layer:
                def block_of(k, first, last):
                    for ii in range(PAIRS if not last else O_LAG):
                        def at(lag):
                            if (first and ii < lag) or (last and ii >= lag):
                                return None
                            return Unit(layer, k, ii - lag, first)
                        iteration(layer, at)
                block_of(0, True, False)
                with eng.Fori(1, B) as k:
                    block_of(k, False, False)
                block_of(B, False, True)
                feed_forward(layer)

        class Unit:
            def __init__(self, layer, k, offset, first):
                self.g = UNITS * layer + PAIRS * k + offset
                self.pair = offset % PAIRS
                self.two, self.four = offset % 2, offset % 4
                self.fours = (UNITS // 4) * layer + (PAIRS // 4) * k + offset // 4
                self.batch = k + offset // PAIRS
                self.batches = B * layer + self.batch
                self.in_layer = offset if first else 99

            def reuses(self, n):
                return self.in_layer >= n

        block = ctx.enter_context(nc.Block())

        @block.sync
        def _(sp):
            for dst, src in ((base[:], rotary.rearrange("a p n -> p a n")), (sq_q[:, 0, :NT * GK], window_mask),
                             (scales[:, 0], q_scale.rearrange("(o l) d -> o l d", o=1).broadcast_to([P, DEPTH, DH])),
                             (scales[:, 1], k_scale.rearrange("(o l) d -> o l d", o=1).broadcast_to([P, DEPTH, DH]))):
                sp.dma_start(dst, src).then_inc(consts_loaded, 16)

            def iteration(layer, at):
                u = at(0)
                if u is None:
                    return
                if u.in_layer == 0:
                    sp.wait_ge(projected, UNITS * layer + 1)
                    sp.dma_start(wqkv[:], w_qkv[bass.ds(layer, 1)].rearrange("o c (a h d) -> (o c) a h d", a=3, d=P)) \
                        .then_inc(att_w_loaded, 16)
                    sp.dma_start(wo[:], w_o[bass.ds(layer, 1)].rearrange("o (h d) n -> d (o h) n", d=P)) \
                        .then_inc(att_w_loaded, 16)
                    sp.wait_ge(ffn_added, B * layer + 1)
                    sp.dma_start(w1[:], w_1[bass.ds(layer, 1)].rearrange("o c f -> (o c) f")).then_inc(ffn_w_loaded, 16)
                    w2_l = w_2[bass.ds(layer, 1)].rearrange("o f n -> (o f) n")
                    for j, (f0, fn) in enumerate(FB):
                        sp.dma_start(w2[:fn, j, :], w2_l[f0:f0 + fn, :]).then_inc(ffn_w_loaded, 16)
                    sp.dma_start(cols[:], columns[bass.ds(layer, 1)].rearrange("o p c -> (o p) c")) \
                        .then_inc(ffn_w_loaded, 16)
                sp.wait_ge(v_copied, u.g + 1)
                sp.wait_ge(attended, u.g + 1)
                dst = v_grp[:, u.four].rearrange("p (t h) d -> p h t d", h=2)
                src = v_rows[:, u.two]
                done = v_grouped[u.four]
                sp.dma_start(dst[0:W, 0, 1:NT], src[P - W:P, 0:NT - 1]).then_inc(done, 16)
                sp.dma_start(dst[W:GK, 0, :], src[0:GQ, :]).then_inc(done, 16)
                sp.dma_start(dst[0:GK, 1, :], src[W:P, :]).then_inc(done, 16)

            pipeline(sp, iteration, lambda layer: None)

        @block.tensor
        def _(pe):
            pe.wait_ge(consts_set, 8)

            def iteration(layer, at):
                u = at(O_LAG)
                if u is not None:
                    pe.wait_ge(att_t_ready, u.g + 1)
                    if u.pair == 0:
                        pe.wait_ge(att_added, u.batches + 1)
                    pe.matmul(psum[:, OUT, :], wo[:, u.pair, :], att_t[:], start=u.pair == 0,
                              stop=u.pair == PAIRS - 1).then_inc(projected, 1)

                def turn_probs(u, h):
                    pe.wait_ge(weighed[h], u.g + 1)
                    if h == 0:
                        if not (at(T_LAG + 1) is None):
                            pe.wait_ge(k_t_ready, at(T_LAG + 1).g + 1)
                    else:
                        pe.wait_ge(p_t_ready[0], u.g + 1)
                    for t in range(NT):
                        last = pe.transpose(psum[:GK, TURN, t * P:(t + 1) * P],
                                            probs[:, u.two, h, t * GK:(t + 1) * GK], ident[:])
                    last.then_inc(p_turned[h], 1)

                v = at(V_LAG)
                if v is not None:
                    turn_probs(v, 0)
                u = at(S_LAG)
                if u is not None:
                    pe.wait_ge(q_t_ready, u.g + 1)
                    pe.wait_ge(k_t_ready, u.g + 1)
                    for h in range(2):
                        if u.reuses(1):
                            pe.wait_ge(exped[h], u.g)
                        pe.matmul(psum[:, S_A + h, :NT * GK], identb[:], mask[:], start=True, stop=True)
                        for g in range(NG):
                            t, half = g // 2, g % 2
                            last = pe.matmul(psum[GQ * half:GQ * half + GQ, S_A + h, t * GK:(t + 1) * GK],
                                             q_t[:, u.two, g * GQ:(g + 1) * GQ],
                                             k_t[:, u.two, h, g * GQ:g * GQ + GK],
                                             start=False, stop=True, skip_group_check=True)
                        last.then_inc(scored, 1)
                if v is not None:
                    turn_probs(v, 1)
                u = at(0)

                def project(u, part, bank, done):
                    for t in range(NT):
                        last = pe.matmul(psum[:, bank, t * P:(t + 1) * P], xs[:, t * P:(t + 1) * P],
                                         wqkv[:, part, u.pair, :], start=True, stop=True)
                    last.then_inc(done, 1)

                if u is not None:
                    if u.in_layer == 0:
                        pe.wait_ge(att_w_loaded, 32 * layer + 32)
                    if u.pair == 0:
                        pe.wait_ge(shifted, 2 * u.batches + 2)
                    if u.reuses(1):
                        pe.wait_ge(q_products, u.g)
                    project(u, 0, RAW_Q, q_raw)
                if v is not None:
                    pe.wait_ge(v_grouped[v.four], 48 * v.fours + 48)
                    pe.wait_ge(p_t_ready[1], v.g + 1)
                    pe.wait_ge(p_t_ready[0], v.g + 1)
                    if at(1) is not None:
                        pe.wait_ge(v_copied, at(1).g + 1)
                    for h in range(2):
                        for g in range(NG):
                            last = pe.matmul(psum[DH * h:DH * h + DH, V_ATT, g * GQ:(g + 1) * GQ],
                                             v_grp[:, v.four, g, h * DH:(h + 1) * DH],
                                             probs_t[:, h, g * GQ:(g + 1) * GQ], start=True, stop=True)
                    last.then_inc(attended, 1)
                if u is not None:
                    if u.reuses(1):
                        pe.wait_ge(k_products, u.g + 1)
                    project(u, 1, RAW_K, k_raw)
                w = at(T_LAG)
                if w is not None:
                    pe.wait_ge(q_rotated, w.g + 1)
                    if w.reuses(1):
                        pe.wait_ge(q_t_ready, w.g)
                    for t in range(NT):
                        last = pe.transpose(psum[:, Q_T, t * P:(t + 1) * P], q_rot[:, w.two, t * P:(t + 1) * P], ident[:])
                    last.then_inc(q_turned, 1)
                    pe.wait_ge(k_rotated, w.g + 1)
                    if v is not None:
                        pe.wait_ge(p_t_ready[1], v.g + 1)
                    elif w.reuses(1):
                        pe.wait_ge(k_t_ready, w.g)
                    for t in range(NT):
                        last = pe.transpose(psum[:, TURN, t * P:(t + 1) * P], k_rot[:, w.two, t * P:(t + 1) * P], ident[:])
                    last.then_inc(k_turned, 1)
                if u is not None:
                    if v is not None:
                        pe.wait_ge(att_t_ready, v.g + 1)
                    elif u.reuses(1):
                        pe.wait_ge(v_copied, u.g)
                    project(u, 2, V_ATT, v_raw)

            def feed_forward(layer):
                with pe.Fori(0, B // 2) as b2:
                    for h in range(2):
                        n = B * layer + 2 * b2 + h
                        pe.wait_ge(f_shifted, 2 * n + 2)
                        pe.matmul(psum[:, h, :], mean_w[:], xf[:, h, :], start=True, stop=True).then_inc(mean_ready, 1)
                    for h in range(2):
                        n = B * layer + 2 * b2 + h
                        pe.wait_ge(squared, n + 1)
                        pe.matmul(psum[:, 2 + h, :], mean_w[:], xsq[:, h, :], start=True, stop=True).then_inc(var_ready, 1)

                def first_product(n, b, h):
                    pe.wait_ge(ln_done, n + 1)
                    for j, (f0, fn) in enumerate(FB):
                        if h:
                            pe.wait_ge(gelu_done, 3 * n - 2 + j)
                        pe.matmul(psum[:fn, j, :], w1[:, FI + f0:FI + f0 + fn], nw[:, bass.ds(b, 1), :],
                                  start=True, stop=True).then_inc(gate_raw, 1)
                    for j, (f0, fn) in enumerate(FB):
                        if h:
                            pe.wait_ge(hid_ready, 3 * n - 2 + j)
                        pe.matmul(psum[:fn, 3 + j, :], w1[:, f0:f0 + fn], nw[:, bass.ds(b, 1), :],
                                  start=True, stop=True).then_inc(hid_raw, 1)

                def second_product(n, h):
                    pe.wait_ge(hid_ready, 3 * n + 3)
                    for j, (f0, fn) in enumerate(FB):
                        last = pe.matmul(psum[:, 6 + h, :], w2[:fn, j, :], hid[:fn, h, j, :], start=j == 0, stop=j == 2)
                    last.then_inc(ffn_raw, 1)

                with pe.Fori(0, B // 2) as b2:
                    n = B * layer + 2 * b2
                    pe.wait_ge(ffn_w_loaded, 80 * layer + 80)
                    pe.wait_ge(ln_done, B * layer + B)
                    pe.wait_ge(ffn_added, n + 1)
                    first_product(n, 2 * b2, 0)
                    first_product(n + 1, 2 * b2 + 1, 1)
                    second_product(n, 0)
                    second_product(n + 1, 1)

            pipeline(pe, iteration, feed_forward)

        @block.scalar
        def _(act):
            act.wait_ge(consts_set, 8)

            def iteration(layer, at):
                v, s, w, u = at(V_LAG), at(S_LAG), at(T_LAG), at(0)
                if v is not None:
                    act.wait_ge(p_turned[1], v.g + 1)
                    if v.reuses(1):
                        act.wait_ge(attended, v.g + 4)
                    act.copy(probs_t[:, 1, :], psum[:GK, TURN, :]).then_inc(p_t_ready[1], 1)

                def exps(s, h):
                    act.wait_ge(biased, 2 * s.g + 1 + h)
                    if s.reuses(2):
                        act.wait_ge(p_turned[h], s.g - 1)
                        act.wait_ge(inverted[h], s.g - 1)
                    for t in range(NT):
                        last = act.activation(probs[:, s.two, h, t * GK:(t + 1) * GK],
                                              psum[:, S_A + h, t * GK:(t + 1) * GK], ACT.Exp,
                                              bias=nbias[:, s.two, h, t:t + 1],
                                              scale=rnorm[:, s.four, 2 * t + h:2 * t + h + 1],
                                              accum_out=den[:, s.two, h, t:t + 1])
                    last.then_inc(exped[h], 1)

                def square(u, raw, bank, dst, summed, done):
                    act.wait_ge(raw, u.g + 1)
                    if u.reuses(2):
                        act.wait_ge(summed, u.g - 1)
                    act.square(dst[:, u.two, :], psum[:, bank, :]).then_inc(done, 1)

                if s is not None:
                    exps(s, 0)
                if u is not None:
                    square(u, q_raw, RAW_Q, sq_q, q_summed, q_squared)
                if s is not None:
                    exps(s, 1)
                if u is not None:
                    square(u, k_raw, RAW_K, sq_k, k_summed, k_squared)
                if w is not None:
                    act.wait_ge(q_turned, w.g + 1)
                    if w.reuses(2):
                        act.wait_ge(scored, 2 * w.g - 2)
                    act.copy(q_t[:, w.two, :], psum[:, Q_T, :]).then_inc(q_t_ready, 1)
                    act.wait_ge(k_turned, w.g + 1)
                    act.copy(k_t[0:DH, w.two, 0, W:], psum[0:DH, TURN, :])
                    act.copy(k_t[DH:P, w.two, 1, W:], psum[DH:P, TURN, :]).then_inc(k_t_ready, 1)
                if u is not None:
                    act.wait_ge(v_raw, u.g + 2)
                    if u.reuses(2):
                        act.wait_ge(v_grouped[(u.four + 2) % 4], 48 * u.fours + (0 if u.four < 2 else 48))
                    act.copy(v_rows[:, u.two].rearrange("p t d -> p (t d)"), psum[:, V_ATT, :]).then_inc(v_copied, 1)

            def feed_forward(layer):
                with act.Fori(0, B // 2) as b2:
                    n = B * layer + 2 * b2
                    for h in range(2):
                        act.wait_ge(centred, n + h + 1)
                        act.square(xsq[:, h, :], xc[:, h, :]).then_inc(squared, 1)
                    for h in range(2):
                        act.wait_ge(var_ready, n + h + 1)
                        act.activation(std[:, h, :], psum[:, 2 + h, :], ACT.Sqrt, bias=eps_col[:]).then_inc(std_ready, 1)
                with act.Fori(0, B // 2) as b2:
                    for h in range(2):
                        n = B * layer + 2 * b2 + h
                        for j, (f0, fn) in enumerate(FB):
                            act.wait_ge(gate_raw, 3 * n + j + 1)
                            act.activation(gate[:fn, h, j, :], psum[:fn, j, :], ACT.Gelu,
                                           bias=cols[:fn, 6 + j:7 + j]).then_inc(gelu_done, 1)

            pipeline(act, iteration, feed_forward)

        @block.vector
        def _(dve):
            for counted in (ffn_added, mean_ready, v_raw, att_added, k_products, projected):
                dve.sem_inc(counted, 1)
            dve.sem_inc(attended, 4)
            dve.memset(mean_w[:], 1.0 / C).then_inc(consts_set, 1)
            dve.memset(eps_col[:], LN_EPS).then_inc(consts_set, 1)
            dve.memset(k_t[:], 0.0).then_inc(consts_set, 1)
            dve.memset(v_grp[:], 0.0).then_inc(consts_set, 1)
            dve.memset(xs[:], 0.0).then_inc(consts_set, 1)
            dve.memset(xf[:], 0.0).then_inc(consts_set, 1)
            dve.wait_ge(consts_loaded, 64)
            dve.tensor_copy(mask[:], sq_q[:, 0, :NT * GK]).then_inc(consts_set, 1)
            dve.tensor_copy(identb[:], ident[:]).then_inc(consts_set, 1)
            dve.wait_ge(consts_set, 8)

            def shift(dst, b, done):
                dve.tensor_copy(dst[0:C // 2, :], sw[0:C // 2, bass.ds(b, 1), :]).then_inc(done, 1)
                dve.tensor_copy(dst[C // 2:C, 1:N], sw[C // 2:C, bass.ds(b, 1), 0:N - 1]).then_inc(done, 1)

            def iteration(layer, at):
                o, v, s, u = at(O_LAG), at(V_LAG), at(S_LAG), at(0)
                if o is not None and o.pair == PAIRS - 1:
                    dve.wait_ge(projected, o.g + 2)
                    xb = sw[:, bass.ds(o.batch, 1), :]
                    dve.tensor_tensor(xb, psum[:, OUT, :].unsqueeze(1), xb, ALU.add).then_inc(att_added, 1)
                if u is not None and u.pair == 0:
                    if u.in_layer == 0:
                        dve.wait_ge(ffn_added, B * layer + 1)
                    dve.wait_ge(v_raw, u.g + 1)
                    shift(xs, u.batch, shifted)
                if v is not None:
                    dve.wait_ge(p_turned[0], v.g + 1)
                    if v.reuses(1):
                        dve.wait_ge(attended, v.g + 4)
                    dve.tensor_copy(probs_t[:, 0, :], psum[:GK, TURN, :]).then_inc(p_t_ready[0], 1)
                if s is not None:
                    for h in range(2):
                        dve.wait_ge(scored, 2 * s.g + 1 + h)
                        if s.reuses(2):
                            dve.wait_ge(exped[h], s.g - 1)
                        dve.tensor_reduce(top[:, s.two, h, :], psum[:, S_A + h, :NT * GK]
                                          .rearrange("p (t k) -> p t k", t=NT), AX.X, ALU.max).then_inc(maxed, 1)
                        dve.wait_ge(maxed, 2 * s.g + 1 + h)
                        dve.scalar_tensor_tensor(
                            out=nbias[:, s.two, h, :], in0=top[:, s.two, h, :], scalar=-1.0,
                            in1=rnorm[:, s.four, 0:8].rearrange("p (t h) -> p h t", h=2)[:, h], op0=ALU.mult,
                            op1=ALU.mult).then_inc(biased, 1)

                def products(u, squared_, bank, cos, sin, which, rotated, done):
                    dve.wait_ge(squared_, u.g + 1)
                    if u.reuses(2):
                        dve.wait_ge(rotated, u.g - 1)
                    dve.tensor_tensor(cos[:, u.two, :], psum[:, bank, :], table[:, 2 * which, :], ALU.mult)
                    dve.tensor_tensor(sin[:, u.two, :], psum[:, bank, :], table[:, 2 * which + 1, :],
                                      ALU.mult).then_inc(done, 1)

                def add_up(u, src, c0, done):
                    dve.tensor_reduce(sums[:, u.two, c0:c0 + 8], src[:, u.two, :].rearrange("p (a d) -> p a d", d=DH),
                                      AX.X, ALU.add).then_inc(done, 1)

                if u is not None:
                    if u.in_layer == 0:
                        dve.wait_ge(tables_ready, 4 * layer + 4)
                    products(u, q_squared, RAW_Q, cos_q, sin_q, 0, q_rotated, q_products)
                if v is not None:
                    dve.wait_ge(attended, v.g + 5)
                    if v.reuses(1):
                        dve.wait_ge(projected, v.g + 1)
                    dve.tensor_copy(att_t[:], psum[:, V_ATT, :]).then_inc(att_t_ready, 1)
                if u is not None:
                    add_up(u, sq_q, 0, q_summed)
                    products(u, k_squared, RAW_K, cos_k, sin_k, 1, k_rotated, k_products)
                    add_up(u, sq_k, 8, k_summed)
                    dve.wait_ge(q_summed, u.g + 1)
                    dve.wait_ge(k_summed, u.g + 1)
                    steps = [11 * u.g]

                    def link(ins):
                        steps[0] = steps[0] + 1
                        ins.then_inc(norm_step, 1)
                        dve.wait_ge(norm_step, steps[0])

                    if u.reuses(4):
                        dve.wait_ge(exped[1], u.g - 3)
                        dve.wait_ge(k_rotated, u.g - 3)
                    x = sums[:, u.two, :]
                    link(dve.tensor_scalar(x, x, 1e-24, None, ALU.max))
                    newton_rsqrt(dve, link, rnorm[:, u.four, :], x, ntmp[:])
                if s is not None:
                    for h in range(2):
                        dve.wait_ge(exped[h], s.g + 1)
                        if s.reuses(2):
                            dve.wait_ge(weighed[h], s.g - 1)
                        dve.reciprocal(rden[:, s.two, h, :], den[:, s.two, h, :]).then_inc(inverted[h], 1)

            def feed_forward(layer):
                with dve.Fori(0, B // 2) as b2:
                    n = B * layer + 2 * b2
                    dve.wait_ge(att_added, B * layer + B + 1)
                    dve.wait_ge(mean_ready, n + 1)
                    for h in range(2):
                        shift(xf[:, h, :], 2 * b2 + h, f_shifted)
                    for h in range(2):
                        dve.wait_ge(mean_ready, n + h + 2)
                        dve.wait_ge(f_shifted, 2 * n + 2 * h + 2)
                        dve.tensor_tensor(xc[:, h, :], xf[:, h, :], psum[:, h, :], ALU.subtract).then_inc(centred, 1)
                    for h in range(2):
                        dve.wait_ge(std_ready, n + h + 1)
                        dve.reciprocal(std[:, h, :], std[:, h, :]).then_inc(f_step, 1)
                    dve.wait_ge(ffn_w_loaded, 80 * layer + 80)
                    for h in range(2):
                        dve.wait_ge(f_step, 4 * (B // 2 * layer + b2) + h + 1)
                        dve.tensor_tensor(xc[:, h, :], xc[:, h, :], std[:, h, :], ALU.mult).then_inc(f_step, 1)
                    for h in range(2):
                        dve.wait_ge(f_step, 4 * (B // 2 * layer + b2) + h + 3)
                        dve.tensor_scalar(nw[:, bass.ds(2 * b2 + h, 1), :], xc[:, h, :].unsqueeze(1), cols[:, 0:1], cols[:, 1:2],
                                          ALU.mult, ALU.add).then_inc(ln_done, 1)
                with dve.Fori(0, B // 2) as b2:
                    for h in range(2):
                        n = B * layer + 2 * b2 + h
                        for j, (f0, fn) in enumerate(FB):
                            dve.wait_ge(gelu_done, 3 * n + j + 1)
                            dve.wait_ge(hid_raw, 3 * n + j + 1)
                            dve.scalar_tensor_tensor(out=hid[:fn, h, j, :], in0=psum[:fn, 3 + j, :],
                                                     scalar=cols[:fn, 3 + j:4 + j], in1=gate[:fn, h, j, :],
                                                     op0=ALU.add, op1=ALU.mult).then_inc(hid_ready, 1)
                    for h in range(2):
                        n = B * layer + 2 * b2 + h
                        dve.wait_ge(ffn_raw, n + 1)
                        xb = sw[:, bass.ds(2 * b2 + h, 1), :]
                        dve.scalar_tensor_tensor(out=xb, in0=psum[:, 6 + h, :].unsqueeze(1), scalar=cols[:, 2:3], in1=xb,
                                                 op0=ALU.add, op1=ALU.add).then_inc(ffn_added, 1)

            pipeline(dve, iteration, feed_forward)

        @block.gpsimd
        def _(pool):
            pool.wait_ge(consts_loaded, 64)

            def iteration(layer, at):
                s, u = at(S_LAG), at(0)
                if u is not None and u.in_layer == 0:
                    pool.wait_ge(k_products, UNITS * layer + 1)
                    for i in range(4):
                        sc = scales[:, i // 2, bass.ds(layer, 1), :].broadcast_to([P, N // DH, DH])
                        pool.tensor_tensor(table[:, i, :].rearrange("p (a d) -> p a d", d=DH),
                                           base[:, i, :].rearrange("p (a d) -> p a d", d=DH), sc,
                                           ALU.mult).then_inc(tables_ready, 1)

                def rotate(u, cos, sin, dst, done):
                    a, b, o = (x[:, u.two, :].rearrange("p (a s d) -> p a s d", s=2, d=DH // 2) for x in (cos, sin, dst))
                    for i in range(2):
                        last = pool.tensor_tensor(o[:, :, i, :], a[:, :, i, :], b[:, :, 1 - i, :], ALU.add)
                    return last

                if u is not None:
                    pool.wait_ge(q_products, u.g + 1)
                    if u.reuses(2):
                        pool.wait_ge(q_turned, u.g - 1)
                    rotate(u, cos_q, sin_q, q_rot, None).then_inc(q_rotated, 1)
                    pool.wait_ge(k_products, u.g + 2)
                    if u.reuses(2):
                        pool.wait_ge(k_turned, u.g - 1)
                    rotate(u, cos_k, sin_k, k_rot, None).then_inc(k_step, 1)
                if s is not None:
                    for h in range(2):
                        pool.wait_ge(inverted[h], s.g + 1)
                        pr = probs[:, s.two, h, :].rearrange("p (t k) -> p t k", t=NT)
                        pool.tensor_tensor(pr, pr, rden[:, s.two, h, :].unsqueeze(2).broadcast_to([P, NT, GK]),
                                           ALU.mult).then_inc(weighed[h], 1)
                if u is not None:
                    pool.wait_ge(k_step, u.g + 1)
                    pool.wait_ge(norm_step, 11 * u.g + 11)
                    kr = k_rot[:, u.two, :].rearrange("p (a d) -> p a d", d=DH)
                    pool.tensor_tensor(kr, kr, rnorm[:, u.four, 8:16].unsqueeze(2).broadcast_to([P, 8, DH]),
                                       ALU.mult).then_inc(k_rotated, 1)

            pipeline(pool, iteration, lambda layer: None)


def finish(nc, out, x_rows, state, ident, psum):
    with ExitStack() as ctx:
        turned = ctx.enter_context(nc.semaphore("out_turned"))
        added = ctx.enter_context(nc.semaphore("out_added"))
        stored = ctx.enter_context(nc.semaphore("out_stored"))
        out_v = out.rearrange("b (t p) c -> p (b t) c", p=P)
        block = ctx.enter_context(nc.Block())

        @block.tensor
        def _(pe):
            for b in range(B):
                for t in range(NT):
                    last = pe.transpose(psum[:, b, t * P:(t + 1) * P], state[:, b * N + t * P:b * N + (t + 1) * P], ident[:])
                last.then_inc(turned, 1)

        @block.vector
        def _(dve):
            for b in range(B):
                dve.wait_ge(turned, b + 1)
                xb = x_rows[:, b * NT:(b + 1) * NT, :].rearrange("p t c -> p (t c)")
                dve.tensor_tensor(xb, psum[:, b, :], xb, ALU.add).then_inc(added, 1)

        @block.sync
        def _(sp):
            for b in range(B):
                sp.wait_ge(added, b + 1)
                sp.dma_start(out_v[:, b * NT:(b + 1) * NT, :], x_rows[:, b * NT:(b + 1) * NT, :]).then_inc(stored, 16)
            sp.wait_ge(stored, 16 * B)


def build(nc, x, wk, bk, wq, bq, wv, bv, wp, bp, w_qkv, q_scale, k_scale, w_o, w_1, w_2, columns, rotary,
          window_mask, causal_masks, ident32, out):
    with ExitStack() as ctx:
        x_rows = ctx.enter_context(nc.sbuf_tensor("x_rows", [P, RT, C], F32))
        state = ctx.enter_context(nc.sbuf_tensor("state", [P, ROWS], F32))
        ident = ctx.enter_context(nc.sbuf_tensor("ident", [P, P], F32))
        psum = ctx.enter_context(nc.psum_tensor("psum", [P, 8, 512], F32))
        layernorm_to_state(nc, x, ident32, x_rows, state, ident, psum)
        causal_attention(nc, wk, bk, wq, bq, wv, bv, wp, bp, causal_masks, x_rows, state, ident, psum)
        layers(nc, w_qkv, q_scale, k_scale, w_o, w_1, w_2, columns, rotary, window_mask, state, ident, psum)
        finish(nc, out, x_rows, state, ident, psum)


def shape_constants():
    import numpy as np
    f = np.float32
    half = np.arange(0, DH, 2, dtype=f)
    inv_freq = (f(1.0) / f(10000.0) ** (half / f(DH))).astype(f)
    t = np.arange(N, dtype=f)
    freqs = (t[:, None] * inv_freq[None, :]).astype(f)
    base = ((half + f(0.4 * DH)) / f(1.4 * DH)).astype(f)
    power = ((t - f(N // 2)) / f(W // 2)).astype(f)
    scale = (base[None, :] ** power[:, None]).astype(f)
    cos, sin = np.cos(freqs), np.sin(freqs)
    inv = (f(1.0) / scale).astype(f)

    def both(a, b):
        one = np.concatenate([a, b], 1).reshape(N // P, P, 1, DH)
        return np.repeat(one, 2, 2).transpose(1, 0, 2, 3).reshape(P, N)

    rotary = np.stack([both(8 * cos * scale, 8 * cos * scale), both(8 * sin * scale, -8 * sin * scale),
                       both(cos * inv, cos * inv), both(sin * inv, -sin * inv)]).astype(f)
    r, c = np.arange(GQ)[:, None], np.arange(GK)[None, :]
    band = (c >= r) & (c <= r + W)
    mask = np.zeros((2, GQ, N // P, GK), f)
    mask[:] = np.where(band, 0.0, -1e20)[None, :, None, :]
    mask[0, :, 0, :] = np.where(band & (c >= W), 0.0, -1e20)
    rows = np.where(np.tril(np.ones((P, P), bool)), 0.0, -1e30)
    causal = np.stack([rows, rows.T], 1)
    return rotary, mask.reshape(P, -1), causal.astype(f)


_NAMES = ["x", "Wk", "bk", "Wq", "bq", "Wv", "bv", "Wp", "bp"]


def inputs_for(inputs):
    import numpy as np
    a = {n: np.asarray(inputs["L0_attn_" + n]) for n in _NAMES}
    f = {n[7:]: np.asarray(v) for n, v in inputs.items() if n.startswith("L0_ffn_")}
    columns = np.zeros((DEPTH, P, 9), np.float32)
    columns[:, :, 0], columns[:, :, 1], columns[:, :, 2] = f["ln_g"], f["ln_b"], f["b2"]
    for j, (f0, fn) in enumerate(FB):
        columns[:, :fn, 3 + j] = f["b1"][:, f0:f0 + fn]
        columns[:, :fn, 6 + j] = f["b1"][:, FI + f0:FI + f0 + fn]
    rotary, mask, causal = shape_constants()
    return {"x": a["x"], "wk": a["Wk"], "bk": a["bk"], "wq": a["Wq"], "bq": a["bq"], "wv": a["Wv"], "bv": a["bv"],
            "wp": a["Wp"], "bp": a["bp"], "w_qkv": f["Wqkv"], "q_scale": f["q_scale"], "k_scale": f["k_scale"],
            "w_o": f["Wo"], "w_1": f["W1"], "w_2": f["W2"], "columns": columns, "rotary": rotary,
            "window_mask": mask, "causal_masks": causal, "ident32": np.eye(P, dtype=np.float32)}


def kernel(**inputs):
    import numpy as np
    import concourse.bacc as bacc
    from concourse.bass_utils import run_bass_kernel_spmd

    arrays = {n: np.ascontiguousarray(v) for n, v in inputs_for(inputs).items()}
    nc = bacc.Bacc("TRN2", target_bir_lowering=False, num_devices=1)
    args = [nc.dram_tensor(n, v.shape, mybir.dt.from_np(v.dtype), kind="ExternalInput").ap() for n, v in arrays.items()]
    out = nc.dram_tensor("out", (B, N, C), F32, kind="ExternalOutput").ap()
    build(nc, *args, out)
    return run_bass_kernel_spmd(nc, [arrays], core_ids=[0]).results[0]["out"]
```

```python
from contextlib import ExitStack

import concourse.bass as bass
from concourse import mybir

F32 = mybir.dt.float32
BF16 = mybir.dt.bfloat16
I32 = mybir.dt.int32
ALU = mybir.AluOpType
ACT = mybir.ActivationFunctionType
AX = mybir.AxisListType

P = 128
B, N, C = 8, 512, 128
ROWS = B * N
RT = ROWS // P
NT = N // P
DEPTH = 6
HEADS, DH = 16, 64
PAIRS = HEADS // 2
INNER = HEADS * DH
W = 32
GQ = 2 * W
GK = GQ + W
NG = N // GQ
FI = 341
FB = [(0, 128), (128, 128), (256, 85)]
UNITS = B * PAIRS
RSQRT_SEED = 0x5F3759DF
LN_EPS = 1e-5


NEWTON = 10


def newton_step(dve, i, y, x, t):
    if i == 0:
        return dve.tensor_scalar(y.bitcast(I32), x.bitcast(I32), -0.5, float(RSQRT_SEED), ALU.mult, ALU.add)
    if i % 3 == 1:
        return dve.scalar_tensor_tensor(out=t, in0=y, scalar=-0.5, in1=y, op0=ALU.mult, op1=ALU.mult)
    if i % 3 == 2:
        return dve.tensor_tensor(t, t, x, ALU.mult)
    return dve.scalar_tensor_tensor(out=y, in0=t, scalar=1.5, in1=y, op0=ALU.add, op1=ALU.mult)


def layernorm_to_state(nc, x, ident_d, x_rows, state, ident, psum):
    with ExitStack() as ctx:
        def sb(name, shape, dt=F32):
            return ctx.enter_context(nc.sbuf_tensor(name, shape, dt))

        def sem(name):
            return ctx.enter_context(nc.semaphore(name))

        centred = sb("ln_centred", [P, RT, C])
        squares = sb("ln_squares", [P, RT, C])
        total = sb("ln_total", [P, RT])
        mean = sb("ln_mean", [P, RT])
        var = sb("ln_var", [P, RT])
        rstd = sb("ln_rstd", [P, RT])
        tmp = sb("ln_tmp", [P, RT])
        x_loaded, ident_loaded = sem("x_loaded"), sem("ident_loaded")
        ln_step, ln_ready, turned, evacuated = sem("ln_step"), sem("ln_ready"), sem("ln_turned"), sem("ln_evacuated")
        x_v = x.rearrange("b (t p) c -> p (b t) c", p=P)
        block = ctx.enter_context(nc.Block())

        @block.sync
        def _(sp):
            sp.dma_start(ident[:], ident_d).then_inc(ident_loaded, 16)
            sp.dma_start(x_rows[:], x_v).then_inc(x_loaded, 16)

        @block.vector
        def _(dve):
            steps = [0]

            def link(ins):
                steps[0] += 1
                ins.then_inc(ln_step, 1)
                dve.wait_ge(ln_step, steps[0])

            dve.wait_ge(x_loaded, 16)
            link(dve.tensor_reduce(total[:], x_rows[:], AX.X, ALU.add))
            link(dve.tensor_scalar(mean[:], total[:], 1.0 / C, None, ALU.mult))
            link(dve.tensor_tensor(centred[:], x_rows[:], mean[:].unsqueeze(2).broadcast_to([P, RT, C]), ALU.subtract))
            link(dve.tensor_tensor(squares[:], centred[:], centred[:], ALU.mult))
            link(dve.tensor_reduce(total[:], squares[:], AX.X, ALU.add))
            link(dve.tensor_scalar(var[:], total[:], 1.0 / C, LN_EPS, ALU.mult, ALU.add))
            for i in range(NEWTON):
                link(newton_step(dve, i, rstd[:], var[:], tmp[:]))
            dve.tensor_tensor(centred[:], centred[:], rstd[:].unsqueeze(2).broadcast_to([P, RT, C]),
                              ALU.mult).then_inc(ln_ready, 1)

        @block.tensor
        def _(pe):
            pe.wait_ge(ident_loaded, 16)
            pe.wait_ge(ln_ready, 1)
            for g in range(RT // 4):
                for j in range(4):
                    last = pe.transpose(psum[:, g % 8, j * P:(j + 1) * P], centred[:, 4 * g + j, :], ident[:])
                last.then_inc(turned, 1)

        @block.scalar
        def _(act):
            for g in range(RT // 4):
                act.wait_ge(turned, g + 1)
                last = act.copy(state[:, g * 512:(g + 1) * 512], psum[:, g % 8, :])
            last.then_inc(evacuated, 1)


def causal_attention(nc, wk, bk, wq, bq, wv, bv, wp, bp, causal_masks, x_rows, state, ident, psum):
    H, D = 16, 8
    PARTS = 3
    KR = D * PARTS * PARTS
    SKEW = 1
    GH = 4
    VW = 32
    LANES = 8
    SCALE = float(D) ** -0.5
    MAX_BANKS, EXP_BANKS, VALUES, MISC_A, MISC_B = (0, 1), (2, 3, 4), 5, 6, 7
    ROW_USES = [[(3, 0)], [(2, 0), (0, 384)], [(1, 0)]]
    KEY_USES = [[(0, 0)], [(1, 0), (3, 384)], [(2, 0)]]
    KEY_COL = {0: 0, 1: 512, 3: 896, 2: 1024}
    with ExitStack() as ctx:
        def sb(name, shape, dt=F32):
            return ctx.enter_context(nc.sbuf_tensor(name, shape, dt))

        def sem(name):
            return ctx.enter_context(nc.semaphore(name))

        w = sb("att_w", [P, 4, P])
        bias = sb("att_bias", [P, 2])
        bias_rows = sb("att_bias_rows", [P, 2, P])
        masks = sb("att_masks", [P, 2, P], BF16)
        identb = sb("att_identb", [P, P], BF16)
        xs = sb("att_x", [P, N])
        f32s = sb("att_qk", [P, 2, N])
        rest = sb("att_rest", [P, 2, N])
        parts = sb("att_parts", [P, 2, PARTS, N], BF16)
        v_rows = sb("att_v", [P, 2, NT, P])
        vx = sb("att_vx", [P, NT, H, VW])
        stacked = sb("att_stacked", [P, 2, 2, H, N], BF16)
        top = sb("att_top", [P, NT, H])
        low = sb("att_low", [P, NT, H])
        neg = sb("att_neg", [P, NT, 2, H], BF16)
        neg_t = sb("att_neg_t", [2 * H, N], BF16)
        probs_t = sb("att_probs_t", [P, LANES, NT * (NT + 1) // 2 * P])
        o_ext = sb("att_o_ext", [P, N])
        rden = sb("att_rden", [P, NT, GH])
        o_rows = sb("att_o_rows", [P, NT, P])
        o_t = sb("att_o_t", [P, N])
        scratch = nc.dram_tensor("att_scratch", (2, 2, P, PARTS * PARTS, N), BF16, kind="Internal").ap()
        scratch_neg = nc.dram_tensor("att_scratch_neg", (2, 2 * H, N), BF16, kind="Internal").ap()

        loaded, consts, ones_set = sem("a_loaded"), sem("a_consts"), sem("a_ones")
        x_copied, q_raw, k_raw, v_raw = sem("a_x_copied"), sem("a_q_raw"), sem("a_k_raw"), sem("a_v_raw")
        q_biased, k_biased, v_ready, vx_ready = sem("a_q_biased"), sem("a_k_biased"), sem("a_v_ready"), sem("a_vx_ready")
        split_step, split = sem("a_split_step"), [sem("a_q_split"), sem("a_k_split")]
        stored = [sem("a_q_stored"), sem("a_k_stored")]
        stacked_in = [[sem("a_low_in_even"), sem("a_low_in_odd")], [sem("a_high_in_even"), sem("a_high_in_odd")]]
        row_scores, row_max = sem("a_row_scores"), sem("a_row_max")
        neg_step, neg_ready, neg_turned, neg_t_ready = (sem("a_neg_step"), sem("a_neg_ready"), sem("a_neg_turned"),
                                                        sem("a_neg_t_ready"))
        neg_stored, neg_in = sem("a_neg_stored"), sem("a_neg_in")
        key_scores, key_exp, valued = sem("a_key_scores"), sem("a_key_exp"), sem("a_valued")
        o_copied, o_turned, o_step, o_ready = sem("a_o_copied"), sem("a_o_turned"), sem("a_o_step"), sem("a_o_ready")
        o_back, o_t_ready, out_made, out_added = sem("a_o_back"), sem("a_o_t_ready"), sem("a_out_made"), sem("a_out_added")
        sw = state[:].rearrange("p (b n) -> p b n", b=B)

        def iterations(eng, iteration):
            iteration(0, 0, True, False, False)
            iteration(1, 1, True, True, False)
            with eng.Fori(1, B // 2) as m:
                for par in range(2):
                    i = eng.alloc_register(f"att_iteration_{par}")
                    eng.reg_mov(i, 2 * m + par)
                    iteration(eng.snap(i), par, True, True, True)
            iteration(B, 0, False, True, True)
            iteration(B + 1, 1, False, False, True)

        def groups_at(slot):
            g, t = slot - SKEW - 5, slot - SKEW - 6
            g = g // GH if g >= 0 and g % GH == 0 else None
            t = t // GH if t >= 0 and t % GH == 0 else None
            return g, t
        SLOTS = H + SKEW + 3

        block = ctx.enter_context(nc.Block())

        @block.sync
        def _(sp):
            def row(v):
                return v.rearrange("(o c) -> o c", o=1).broadcast_to([P, P])
            for dst, src in ((w[:, 0], wq), (w[:, 1], wk), (w[:, 2], wv), (w[:, 3], wp),
                             (bias[:, 0:1], bq.rearrange("(c o) -> c o", o=1)), (bias[:, 1:2], bk.rearrange("(c o) -> c o", o=1)),
                             (bias_rows[:, 0], row(bv)), (bias_rows[:, 1], row(bp)),
                             (rest[:, 0, 0:2 * P], causal_masks.rearrange("p a k -> p (a k)"))):
                sp.dma_start(dst, src).then_inc(loaded, 16)

            def iteration(i, par, prep, pass1, pass2):
                if prep:
                    for j in range(2):
                        sp.wait_ge(split[j], i + 1)
                        dst = scratch[par, j].rearrange("p (a b) n -> p a b n", a=PARTS)
                        for a in range(PARTS):
                            src = parts[:, 0, a:a + 1].broadcast_to([P, PARTS, N]) if j == 0 else parts[:, 1]
                            sp.dma_start(dst[:, a], src).then_inc(stored[j], 16)
                    for j in range(2):
                        sp.wait_ge(stored[j], 48 * i + 48)
                    sp.wait_ge(ones_set, 1)
                    for c in range(2):
                        if pass2:
                            sp.wait_ge(key_scores, 48 * (i - 2) + 24 * (c + 1))
                        for j in range(2):
                            sp.dma_start(stacked[0:KR, par, j, 8 * c:8 * c + 8, :],
                                         scratch[par, j].rearrange("(h d) a n -> (d a) h n", d=D)[:, 8 * c:8 * c + 8]) \
                                .then_inc(stacked_in[c][par], 16)
                if pass1:
                    sp.wait_ge(neg_t_ready, i)
                    sp.dma_start(scratch_neg[1 - par], neg_t[:]).then_inc(neg_stored, 16)
                    sp.wait_ge(neg_stored, 16 * i)
                    sp.dma_start(stacked[KR:KR + 2, 1 - par, 0], scratch_neg[1 - par].rearrange("(a h) n -> a h n", a=2)) \
                        .then_inc(neg_in, 16)

            iterations(sp, iteration)

        @block.tensor
        def _(pe):
            pe.wait_ge(loaded, 144)
            pe.wait_ge(consts, 5)

            def iteration(i, par, prep, pass1, pass2):
                n1, n2 = i - 1, i - 2

                def prepare_qk():
                    pe.wait_ge(x_copied, i + 1)
                    pe.wait_ge(v_ready, i)
                    if pass2:
                        pe.wait_ge(o_t_ready, i - 1)
                        pe.wait_ge(out_added, i - 1)
                    pe.wait_ge(k_biased, i)
                    if pass1:
                        pe.wait_ge(neg_t_ready, i - 1)
                    pe.matmul(psum[:, MISC_A, :], w[:, 0], xs[:], start=True, stop=True).then_inc(q_raw, 1)
                    pe.matmul(psum[:, MISC_B, :], w[:, 1], xs[:], start=True, stop=True).then_inc(k_raw, 1)

                def prepare_v():
                    pe.wait_ge(q_biased, i + 1)
                    for t in range(NT):
                        last = pe.matmul(psum[:, MISC_A, t * P:(t + 1) * P], xs[:, t * P:(t + 1) * P], w[:, 2],
                                         start=True, stop=True)
                    last.then_inc(v_raw, 1)

                def scores(n, h, p_, uses, banks, free, done, rows, mask, spans):
                    for j, use in enumerate(uses):
                        free(j)
                        bank = banks(j)
                        for t, c0 in use:
                            (lhs, l0), (rhs, r0), width, diag = spans(t)
                            for a, b, on_mask in ((0, diag, False), (diag, diag + P, True), (diag + P, width, False)):
                                if a >= b:
                                    continue
                                dst = psum[:, bank, c0 + a:c0 + b]
                                if on_mask:
                                    pe.matmul(dst, identb[:], mask, start=True, stop=True)
                                last = pe.matmul(dst, stacked[0:rows, p_, lhs, h, l0:l0 + P],
                                                 stacked[0:rows, p_, rhs, h, r0 + a:r0 + b],
                                                 start=not on_mask, stop=True, skip_group_check=on_mask)
                        last.then_inc(done, 1)

                def pass_one(h):
                    if h % 8 == 0:
                        pe.wait_ge(stacked_in[h // 8][1 - par], 16 * (n1 - (1 - par)) + 32)

                    def free(j):
                        if 3 * h + j >= 2:
                            pe.wait_ge(row_max, 48 * n1 + 3 * h + j - 1)
                        else:
                            pe.wait_ge(row_max, 48 * n1)
                    scores(n1, h, 1 - par, ROW_USES, lambda j: MAX_BANKS[(3 * h + j) % 2], free, row_scores, KR,
                           masks[:, 0], lambda t: ((0, t * P), (1, 0), (t + 1) * P, t * P))

                def pass_two(h):
                    if h == 0:
                        pe.wait_ge(neg_in, 16 * n2 + 16)
                    scores(n2, h, par, KEY_USES, lambda j: EXP_BANKS[j],
                           lambda j: pe.wait_ge(key_exp, 48 * n2 + 3 * h + j - 1) if 3 * h + j > 2 else
                           pe.wait_ge(key_exp, 48 * n2 + 1), key_scores, KR + 2,
                           masks[:, 1], lambda t: ((1, t * P), (0, t * P), N - t * P, 0))

                def values(g):
                    pe.wait_ge(vx_ready, n2 + 1)
                    pe.wait_ge(key_exp, 48 * n2 + 12 * g + 13)
                    pe.wait_ge(o_copied, 4 * n2 + g + 1)
                    for t in range(NT):
                        for j in range(GH):
                            h = GH * g + j
                            last = pe.matmul(psum[VW * j:VW * j + VW, VALUES, t * P:N], vx[:, t, h, :],
                                             probs_t[:, h % LANES, KEY_COL[t]:KEY_COL[t] + N - t * P],
                                             start=t == 0, stop=t == NT - 1, skip_group_check=True)
                    last.then_inc(valued, 1)

                def turn_output(g):
                    pe.wait_ge(o_copied, 4 * n2 + g + 2)
                    if g == 0 and prep:
                        pe.wait_ge(v_ready, i + 1)
                    if g == 1 and prep:
                        pe.wait_ge(k_biased, i + 1)
                    if g == 3 and pass1:
                        pe.wait_ge(neg_t_ready, i)
                    if g >= 2:
                        pe.wait_ge(o_ready, 4 * n2 + g)
                    for t in range(NT):
                        last = pe.transpose(psum[:, MISC_A + g % 2, t * P:(t + 1) * P], o_ext[:, t * P:(t + 1) * P],
                                            ident[:])
                    last.then_inc(o_turned, 1)

                def turn_maxima():
                    pe.wait_ge(neg_ready, n1 + 1)
                    if pass2:
                        pe.wait_ge(o_ready, 4 * n2 + 3)
                    if prep:
                        pe.wait_ge(k_biased, i + 1)
                    turned = psum[0:2 * H, MISC_B, 0:N // 2].bitcast(BF16)
                    for t in range(NT):
                        last = pe.transpose(turned[:, t * P:(t + 1) * P], neg[:, t].rearrange("p a h -> p (a h)"),
                                            identb[:])
                    last.then_inc(neg_turned, 1)

                for s in range(SLOTS):
                    if s == 0 and prep:
                        prepare_qk()
                    if pass1 and s < H:
                        pass_one(s)
                    if s == 1 and prep:
                        prepare_v()
                    if pass2 and SKEW <= s < H + SKEW:
                        pass_two(s - SKEW)
                    g, t = groups_at(s)
                    if pass1 and s == H + 1:
                        turn_maxima()
                    if pass2 and g is not None:
                        values(g)
                    if pass2 and t is not None:
                        turn_output(t)
                if pass2:
                    pe.wait_ge(o_ready, 4 * n2 + 5)
                    for t in range(NT):
                        last = pe.transpose(psum[:, MISC_A, t * P:(t + 1) * P], o_rows[:, t, :], ident[:])
                    last.then_inc(o_back, 1)
                    pe.wait_ge(o_t_ready, n2 + 2)
                    for t in range(NT):
                        last = pe.matmul(psum[:, MISC_B, t * P:(t + 1) * P], o_t[:, t * P:(t + 1) * P], w[:, 3],
                                         start=True, stop=True)
                    last.then_inc(out_made, 1)

            iterations(pe, iteration)

        @block.scalar
        def _(act):
            act.wait_ge(loaded, 144)

            def iteration(i, par, prep, pass1, pass2):
                n2 = i - 2
                if prep:
                    for j, (raw, done) in enumerate(((q_raw, q_biased), (k_raw, k_biased))):
                        act.wait_ge(raw, i + 1)
                        act.wait_ge(split[j], i)
                        act.activation(f32s[:, j], psum[:, MISC_A + j, :], ACT.Identity,
                                       bias=bias[:, j:j + 1]).then_inc(done, 1)
                for s in range(SLOTS):
                    if pass2 and SKEW <= s < H + SKEW:
                        h = s - SKEW
                        if h % GH == 0:
                            act.wait_ge(valued, 4 * n2 + h // GH + 1)
                        for j, c0, c in ((0, 0, 512), (1, 512, 512), (2, 1024, 256)):
                            act.wait_ge(key_scores, 48 * n2 + 3 * h + j + 1)
                            act.activation(probs_t[:, h % LANES, c0:c0 + c], psum[:, EXP_BANKS[j], 0:c], ACT.Exp,
                                           scale=SCALE).then_inc(key_exp, 1)
                    g, t = groups_at(s)
                    if pass1 and s == H + 1:
                        act.wait_ge(neg_turned, i)
                        if i is not None:
                            act.wait_ge(neg_stored, 16 * (i - 1))
                        act.copy(neg_t[:], psum[0:2 * H, MISC_B, 0:N // 2].bitcast(BF16)).then_inc(neg_t_ready, 1)
                    if pass2 and g is not None:
                        act.wait_ge(valued, 4 * n2 + g + 1 + 2)
                        act.wait_ge(o_turned, 4 * n2 + g + 1)
                        act.copy(o_ext[:], psum[:, VALUES, :]).then_inc(o_copied, 1)
                if pass2:
                    act.wait_ge(o_back, n2 + 2)
                    act.wait_ge(out_made, n2 + 1)
                    act.copy(o_t[:], psum[:, MISC_A, :]).then_inc(o_t_ready, 1)

            iterations(act, iteration)

        @block.vector
        def _(dve):
            dve.memset(vx[:], 0.0).then_inc(consts, 1)
            dve.wait_ge(consts, 1)
            dve.memset(vx[:, :, :, D:D + 1], 1.0).then_inc(consts, 1)
            for counted in (o_turned, out_made, o_back, o_ready, key_exp, o_copied, o_t_ready, out_added):
                dve.sem_inc(counted, 1)
            dve.sem_inc(valued, 2)
            dve.wait_ge(loaded, 144)
            dve.tensor_tensor(x_rows[:], x_rows[:], bias_rows[:, 1].unsqueeze(1).broadcast_to([P, RT, P]),
                              ALU.add).then_inc(consts, 1)
            dve.tensor_copy(masks[:].rearrange("p a k -> p (a k)"), rest[:, 0, 0:2 * P]).then_inc(consts, 1)
            dve.tensor_copy(identb[:], ident[:]).then_inc(consts, 1)
            dve.wait_ge(consts, 5)

            def iteration(i, par, prep, pass1, pass2):
                n1, n2 = i - 1, i - 2

                def split_parts(j):
                    dve.wait_ge((q_biased, k_biased)[j], i + 1)
                    dve.wait_ge(stored[j], 48 * i)
                    steps = [8 * i + 4 * j]

                    def link(ins):
                        steps[0] = steps[0] + 1
                        ins.then_inc(split_step, 1)
                        dve.wait_ge(split_step, steps[0])

                    link(dve.tensor_copy(parts[:, j, 0], f32s[:, j]))
                    link(dve.tensor_tensor(rest[:, j], f32s[:, j], parts[:, j, 0], ALU.subtract))
                    link(dve.tensor_copy(parts[:, j, 1], rest[:, j]))
                    link(dve.tensor_tensor(rest[:, j], rest[:, j], parts[:, j, 1], ALU.subtract))
                    dve.tensor_copy(parts[:, j, 2], rest[:, j]).then_inc(split[j], 1)

                def row_maxima(h):
                    for j, use in enumerate(ROW_USES):
                        dve.wait_ge(row_scores, 48 * n1 + 3 * h + j + 1)
                        if h == 0 and j == 0:
                            dve.wait_ge(neg_ready, n1)
                        for t, c0 in use:
                            last = dve.tensor_reduce(top[:, t, h:h + 1],
                                                     psum[:, MAX_BANKS[(3 * h + j) % 2], c0:c0 + (t + 1) * P], AX.X, ALU.max)
                        last.then_inc(row_max, 1)

                if pass2:
                    dve.wait_ge(valued, 4 * n2 + 2)
                    dve.tensor_copy(vx[:, :, :, 0:D], v_rows[:, par].rearrange("p t (h d) -> p t h d", d=D)) \
                        .then_inc(vx_ready, 1)
                if prep:
                    dve.wait_ge(v_raw, i)
                    dve.tensor_copy(xs[:].unsqueeze(1), sw[:, bass.ds(i, 1), :]).then_inc(x_copied, 1)
                for s in range(SLOTS):
                    if pass1 and s < H:
                        row_maxima(s)
                    if prep and s in (0, 1):
                        split_parts(s)
                    if prep and s == 1:
                        dve.wait_ge(v_raw, i + 1)
                        if pass2:
                            dve.wait_ge(vx_ready, n2 + 1)
                        dve.tensor_tensor(v_rows[:, par], psum[:, MISC_A, :].rearrange("p (t c) -> p t c", t=NT),
                                          bias_rows[:, 0].unsqueeze(1).broadcast_to([P, NT, P]), ALU.add) \
                            .then_inc(v_ready, 1)
                    if pass1 and s == H - 1:
                        dve.wait_ge(row_max, 48 * n1 + 48)
                        dve.wait_ge(neg_turned, n1)
                        dve.tensor_scalar(neg[:, :, 0], top[:], -1.0, None, ALU.mult).then_inc(neg_step, 1)
                        dve.wait_ge(neg_step, 2 * n1 + 1)
                        dve.tensor_tensor(low[:], top[:], neg[:, :, 0], ALU.add).then_inc(neg_step, 1)
                        dve.wait_ge(neg_step, 2 * n1 + 2)
                        dve.tensor_scalar(neg[:, :, 1], low[:], -1.0, None, ALU.mult).then_inc(neg_ready, 1)
                    g, t = groups_at(s)
                    if pass2 and t is not None:
                        dve.wait_ge(o_turned, 4 * n2 + t + 2)
                        dve.wait_ge(o_ready, 4 * n2 + t + 1)
                        src = psum[:, MISC_A + t % 2, :].rearrange("p (t h c) -> p t h c", t=NT, h=GH)
                        dve.reciprocal(rden[:], src[:, :, :, D]).then_inc(o_step, 1)
                        dve.wait_ge(o_step, 4 * n2 + t + 1)
                        if t == 0:
                            dve.wait_ge(o_back, n2 + 1)
                        dve.tensor_tensor(o_rows[:, :, GH * D * t:GH * D * (t + 1)].rearrange("p t (h d) -> p t h d", d=D),
                                          src[:, :, :, 0:D], rden[:].unsqueeze(3).broadcast_to([P, NT, GH, D]), ALU.mult) \
                            .then_inc(o_ready, 1)
                if pass2:
                    dve.wait_ge(out_made, n2 + 2)
                    xb = x_rows[:, bass.ds(NT * n2, NT), :]
                    dve.tensor_tensor(xb, psum[:, MISC_B, :].rearrange("p (t c) -> p t c", t=NT), xb, ALU.add) \
                        .then_inc(out_added, 1)

            iterations(dve, iteration)

        @block.gpsimd
        def _(pool):
            pool.memset(stacked[64:96, :, 1], 1.0).then_inc(ones_set, 1)


def layers(nc, w_qkv, q_scale, k_scale, w_o, w_1, w_2, columns, rotary, window_mask, state, ident, psum):
    LAST_LAG = 4
    V_GROUP_LAG = 0
    CONSTS = 7
    ATT_LOADS, FFN_LOADS = 16 * 2, 16 * (2 + len(FB))
    with ExitStack() as ctx:
        def sb(name, shape, dt=F32):
            return ctx.enter_context(nc.sbuf_tensor(name, shape, dt))

        def sem(name):
            return ctx.enter_context(nc.semaphore(name))

        wqkv = sb("wqkv", [P, 3, PAIRS, P])
        wo = sb("wo", [P, PAIRS, P])
        w1 = sb("w1", [P, 2 * FI])
        w2 = sb("w2", [P, len(FB), P])
        cols = sb("cols", [P, 9])
        base = sb("rotary_base", [P, 4, N])
        table = sb("rotary_table", [P, 4, N])
        scales = sb("scales", [P, 2, DEPTH, DH])
        mask = sb("mask", [P, NT * GK], BF16)
        identb = sb("identb", [P, P], BF16)
        mean_w = sb("mean_w", [P, P])
        eps_col = sb("eps_col", [P, 1])
        xs = sb("xs", [P, N])
        sq_q = sb("sq_q", [P, 2, N])
        sq_k = sb("sq_k", [P, 2, N])
        products_of = sb("rotary_products", [P, 4, 2, N])
        cos_q, sin_q, cos_k, sin_k = (products_of[:, i] for i in range(4))
        q_rot, k_rot = sb("q_rot", [P, 2, N]), sb("k_rot", [P, 2, N])
        sums = sb("norm_sums", [P, 2, 16])
        rnorm = sb("rnorm", [P, 4, 16])
        ntmp = sb("norm_tmp", [P, 16])
        q_t = sb("q_t", [P, 2, N])
        k_t = sb("k_t", [P, 2, 2, W + N])
        v_rows = sb("v_rows", [P, 2, NT, P])
        v_grp = sb("v_grp", [GK, 4, NG, P])
        top = sb("score_max", [P, 2, 2, NT])
        nbias = sb("score_nbias", [P, 2, 2, NT])
        den = sb("den", [P, 2, 2, NT])
        rden = sb("rden", [P, 2, 2, NT])
        probs = sb("probs", [P, 2, 2, NT * GK])
        probs_t = sb("probs_t", [GK, 2, N])
        att_t = sb("att_t", [P, N])
        xsq = sb("xsq", [P, 2, N])
        var = sb("var", [P, RT])
        rstd = sb("rstd", [P, RT])
        ftmp = sb("rstd_tmp", [P, RT])
        work = sb("work", [P, B, N])
        ones = sb("ones", [P, P])
        rstd_rows = sb("rstd_rows", [P, 2, N])
        xf = sb("xf", [P, B, N])
        gate = xf[:, 0:2 * len(FB), :].rearrange("p (h j) n -> p h j n", h=2)
        hid = products_of[:, 0:3].rearrange("p j h n -> p h j n")

        RAW_Q, RAW_K, V_ATT, TURN_A, S_A, S_B, TURN_B, OUT = range(8)
        TURN_BANKS, P_BANKS = (TURN_A, TURN_B), (TURN_A, TURN_B)
        SPREAD, FFN_OUT = 6, 7

        consts_loaded, consts_set = sem("consts_loaded"), sem("consts_set")
        att_w_loaded, ffn_w_loaded, tables_ready = sem("att_w_loaded"), sem("ffn_w_loaded"), sem("tables_ready")
        shifted = sem("shifted")
        raw = [sem("q_raw"), sem("k_raw"), sem("v_raw")]
        squared = [sem("q_squared"), sem("k_squared")]
        multiplied = [sem("q_multiplied"), sem("k_multiplied")]
        summed = [sem("q_summed"), sem("k_summed")]
        normed = [sem(f"norm_step{i}") for i in range(NEWTON + 1)]
        rotated = [sem("q_rotated"), sem("k_rotated")]
        k_scaled = sem("k_scaled")
        turned = [sem("q_turned"), sem("k_turned")]
        t_ready = [sem("q_t_ready"), sem("k_t_ready")]
        v_copied = sem("v_copied")
        v_grouped = [sem(f"v_grouped{i}") for i in range(4)]
        scored = [sem("scored_a"), sem("scored_b")]
        maxed = [sem("maxed_a"), sem("maxed_b")]
        biased = [sem("biased_a"), sem("biased_b")]
        exped = [sem("exped_a"), sem("exped_b")]
        inverted = [sem("inverted_a"), sem("inverted_b")]
        weighed = [sem("weighed_a"), sem("weighed_b")]
        p_turned = [sem("p_turned_a"), sem("p_turned_b")]
        p_t_ready = [sem("p_t_ready_a"), sem("p_t_ready_b")]
        attended, att_t_ready, projected, att_added = sem("attended"), sem("att_t_ready"), sem("projected"), sem("att_added")
        f_shifted, mean_ready, centred = sem("f_shifted"), sem("mean_ready"), sem("f_centred")
        f_squared, var_ready, var_copied = sem("f_squared"), sem("var_ready"), sem("var_copied")
        rstd_step, rstd_spread, scaled, ln_done = sem("rstd_step"), sem("rstd_spread"), sem("f_scaled"), sem("ln_done")
        gate_raw, hid_raw, gelu_done, hid_ready = sem("gate_raw"), sem("hid_raw"), sem("gelu_done"), sem("hid_ready")
        pad_zeroed = sem("pad_zeroed")
        rstd_rows_ready = sem("rstd_rows_ready")
        ffn_raw, ffn_added = sem("ffn_raw"), sem("ffn_added")
        sw = state[:].rearrange("p (b n) -> p b n", b=B)

        def pipeline(eng, iteration, feed_forward):
            with eng.Fori(0, DEPTH) as layer:
                def block_of(k, first, last):
                    for ii in range(PAIRS if not last else LAST_LAG):
                        def at(lag):
                            if (first and ii < lag) or (last and ii >= lag):
                                return None
                            return Unit(layer, k, ii - lag, first)
                        iteration(layer, at)
                block_of(0, True, False)
                with eng.Fori(1, B) as k:
                    block_of(k, False, False)
                block_of(B, False, True)
                feed_forward(layer)

        def over_batches(eng, layer, lag, iteration):
            def steps(b2, first, last):
                for h in range(lag if last else 2):
                    def at(l):
                        if (first and h < l) or (last and h >= l):
                            return None
                        return Batch(layer, b2, h - l, first)
                    iteration(at)
            steps(0, True, False)
            with eng.Fori(1, B // 2) as b2:
                steps(b2, False, False)
            steps(B // 2, False, True)

        class Batch:
            def __init__(self, layer, b2, offset, first):
                self.b = 2 * b2 + offset
                self.n = B * layer + 2 * b2 + offset
                self.two = offset % 2
                self.in_layer = offset if first else 99

            def reuses(self, n):
                return self.in_layer >= n

        class Unit:
            def __init__(self, layer, k, offset, first):
                self.layer = layer
                self.g = UNITS * layer + PAIRS * k + offset
                self.pair = offset % PAIRS
                self.two, self.four = offset % 2, offset % 4
                self.fours = (UNITS // 4) * layer + (PAIRS // 4) * k + offset // 4
                self.batch = k + offset // PAIRS
                self.batches = B * layer + self.batch
                self.in_layer = offset if first else 99

            def reuses(self, n):
                return self.in_layer >= n

        def bank_free(eng, *readers):
            for done, unit in readers:
                if unit is not None:
                    eng.wait_ge(done, unit.g + 1)
                    return

        block = ctx.enter_context(nc.Block())

        @block.sync
        def _(sp):
            for dst, src in ((base[:], rotary.rearrange("a p n -> p a n")), (sq_q[:, 0, :NT * GK], window_mask),
                             (scales[:, 0], q_scale.rearrange("(o l) d -> o l d", o=1).broadcast_to([P, DEPTH, DH])),
                             (scales[:, 1], k_scale.rearrange("(o l) d -> o l d", o=1).broadcast_to([P, DEPTH, DH]))):
                sp.dma_start(dst, src).then_inc(consts_loaded, 16)

            def iteration(layer, at):
                u = at(0)
                if u is not None and u.in_layer == 0:
                    sp.wait_ge(projected, UNITS * layer + 1)
                    sp.dma_start(wqkv[:], w_qkv[bass.ds(layer, 1)].rearrange("o c (a h d) -> (o c) a h d", a=3, d=P)) \
                        .then_inc(att_w_loaded, 16)
                    sp.dma_start(wo[:], w_o[bass.ds(layer, 1)].rearrange("o (h d) n -> d (o h) n", d=P)) \
                        .then_inc(att_w_loaded, 16)
                    sp.wait_ge(ffn_added, B * layer + 1)
                    sp.dma_start(w1[:], w_1[bass.ds(layer, 1)].rearrange("o c f -> (o c) f")).then_inc(ffn_w_loaded, 16)
                    w2_l = w_2[bass.ds(layer, 1)].rearrange("o f n -> (o f) n")
                    for j, (f0, fn) in enumerate(FB):
                        sp.dma_start(w2[:fn, j, :], w2_l[f0:f0 + fn, :]).then_inc(ffn_w_loaded, 16)
                    sp.dma_start(cols[:], columns[bass.ds(layer, 1)].rearrange("o p c -> (o p) c")) \
                        .then_inc(ffn_w_loaded, 16)
                u = at(V_GROUP_LAG)
                if u is None:
                    return
                sp.wait_ge(v_copied, u.g + 1)
                sp.wait_ge(attended, u.g + 1)
                dst = v_grp[:, u.four].rearrange("p (t h) d -> p h t d", h=2)
                src = v_rows[:, u.two]
                done = v_grouped[u.four]
                sp.dma_start(dst[0:W, 0, 1:NT], src[P - W:P, 0:NT - 1]).then_inc(done, 16)
                sp.dma_start(dst[W:GK, 0, :], src[0:GQ, :]).then_inc(done, 16)
                sp.dma_start(dst[0:GK, 1, :], src[W:P, :]).then_inc(done, 16)

            pipeline(sp, iteration, lambda layer: None)

        @block.tensor
        def _(pe):
            pe.wait_ge(consts_set, CONSTS)

            def project(u, part, *readers):
                if u is None:
                    return
                bank = (RAW_Q, RAW_K, V_ATT)[part]
                if u.in_layer == 0:
                    pe.wait_ge(att_w_loaded, ATT_LOADS * (u.layer + 1))
                if u.pair == 0:
                    pe.wait_ge(shifted, u.batches + 1)
                bank_free(pe, *readers)
                for t in range(NT):
                    last = pe.matmul(psum[:, bank, t * P:(t + 1) * P], xs[:, t * P:(t + 1) * P],
                                     wqkv[:, part, u.pair, :], start=True, stop=True)
                last.then_inc(raw[part], 1)

            def turn(u, j, *readers):
                if u is None:
                    return
                pe.wait_ge((rotated[0], k_scaled)[j], u.g + 1)
                bank_free(pe, *readers)
                src = (q_rot, k_rot)[j]
                for t in range(NT):
                    last = pe.transpose(psum[:, TURN_BANKS[j], t * P:(t + 1) * P], src[:, u.two, t * P:(t + 1) * P], ident[:])
                last.then_inc(turned[j], 1)

            def scores(u, h, *readers):
                if u is None:
                    return
                pe.wait_ge(t_ready[0], u.g + 1)
                pe.wait_ge(t_ready[1], u.g + 1)
                bank_free(pe, *readers)
                pe.matmul(psum[:, S_A + h, :NT * GK], identb[:], mask[:], start=True, stop=True)
                for g in range(NG):
                    t, half = g // 2, g % 2
                    last = pe.matmul(psum[GQ * half:GQ * half + GQ, S_A + h, t * GK:(t + 1) * GK],
                                     q_t[:, u.two, g * GQ:(g + 1) * GQ], k_t[:, u.two, h, g * GQ:g * GQ + GK],
                                     start=False, stop=True, skip_group_check=True)
                last.then_inc(scored[h], 1)

            def turn_probs(u, h, *readers):
                if u is None:
                    return
                pe.wait_ge(weighed[h], u.g + 1)
                bank_free(pe, *readers)
                for t in range(NT):
                    last = pe.transpose(psum[:GK, P_BANKS[h], t * P:(t + 1) * P],
                                        probs[:, u.two, h, t * GK:(t + 1) * GK], ident[:])
                last.then_inc(p_turned[h], 1)

            def values(u, *readers):
                if u is None:
                    return
                pe.wait_ge(v_grouped[u.four], 48 * u.fours + 48)
                pe.wait_ge(p_t_ready[0], u.g + 1)
                pe.wait_ge(p_t_ready[1], u.g + 1)
                bank_free(pe, *readers)
                for h in range(2):
                    for g in range(NG):
                        last = pe.matmul(psum[DH * h:DH * h + DH, V_ATT, g * GQ:(g + 1) * GQ],
                                         v_grp[:, u.four, g, h * DH:(h + 1) * DH],
                                         probs_t[:, h, g * GQ:(g + 1) * GQ], start=True, stop=True)
                last.then_inc(attended, 1)

            def project_out(u):
                if u is None:
                    return
                pe.wait_ge(att_t_ready, u.g + 1)
                if u.pair == 0:
                    pe.wait_ge(att_added, u.batches + 1)
                pe.matmul(psum[:, OUT, :], wo[:, u.pair, :], att_t[:], start=u.pair == 0,
                          stop=u.pair == PAIRS - 1).then_inc(projected, 1)

            def iteration(layer, at):
                project(at(0), 1, (multiplied[1], at(1)))
                values(at(4), (v_copied, at(1)), (att_t_ready, at(5)))
                scores(at(2), 1, (exped[1], at(3)))
                project(at(0), 0, (multiplied[0], at(1)))
                turn(at(1), 0, (p_t_ready[0], at(4)), (t_ready[0], at(2)))
                project(at(0), 2, (att_t_ready, at(4)), (v_copied, at(1)))
                project_out(at(4))
                turn_probs(at(3), 1, (t_ready[1], at(2)), (p_t_ready[1], at(4)))
                turn_probs(at(3), 0, (t_ready[0], at(1)), (p_t_ready[0], at(4)))
                scores(at(2), 0, (exped[0], at(3)))
                turn(at(1), 1, (p_t_ready[1], at(3)), (t_ready[1], at(2)))

            def feed_forward(layer):
                def statistics(at):
                    b, c = at(0), at(2)
                    if b is not None:
                        pe.wait_ge(f_shifted, b.n + 1)
                        if b.reuses(2):
                            pe.wait_ge(centred, b.n - 1)
                        pe.matmul(psum[:, b.two, :], mean_w[:], xf[:, bass.ds(b.b, 1), :], start=True, stop=True) \
                            .then_inc(mean_ready, 1)
                    if c is not None:
                        pe.wait_ge(f_squared, c.n + 1)
                        pe.wait_ge(var_copied, c.n + 1)
                        for t in range(NT):
                            last = pe.matmul(psum[:, 2 + c.two, t:t + 1], xsq[:, c.two, t * P:(t + 1) * P], mean_w[:, 0:1],
                                             start=True, stop=True)
                        last.then_inc(var_ready, 1)

                def spread(b):
                    pe.wait_ge(rstd_rows_ready, b.n + 1)
                    if b.reuses(1):
                        pe.wait_ge(scaled, b.n)
                    for t in range(NT):
                        last = pe.transpose(psum[:, SPREAD, t * P:(t + 1) * P], rstd_rows[:, b.two, t * P:(t + 1) * P], ident[:])
                    last.then_inc(rstd_spread, 1)

                def products(at):
                    a, b, c = at(0), at(1), at(2)
                    if b is not None:
                        pe.wait_ge(ln_done, b.n + 1)
                        for j, (f0, fn) in enumerate(FB):
                            if b.reuses(1):
                                pe.wait_ge(gelu_done, 3 * b.n - 2 + j)
                            pe.matmul(psum[:fn, j, :], w1[:, FI + f0:FI + f0 + fn], work[:, bass.ds(b.b, 1), :],
                                      start=True, stop=True).then_inc(gate_raw, 1)
                    if a is not None:
                        spread(a)
                    if b is not None:
                        for j, (f0, fn) in enumerate(FB):
                            if b.reuses(1):
                                pe.wait_ge(hid_ready, 3 * b.n - 2 + j)
                            pe.matmul(psum[:fn, 3 + j, :], w1[:, f0:f0 + fn], work[:, bass.ds(b.b, 1), :],
                                      start=True, stop=True).then_inc(hid_raw, 1)
                    if c is not None:
                        pe.wait_ge(hid_ready, 3 * c.n + 3)
                        pe.wait_ge(ffn_added, c.n + 1)
                        for j, (f0, fn) in enumerate(FB):
                            last = pe.matmul(psum[:, FFN_OUT, :], w2[:fn, j, :], hid[:fn, c.two, j, :], start=j == 0, stop=j == 2)
                        last.then_inc(ffn_raw, 1)

                over_batches(pe, layer, 2, statistics)
                pe.wait_ge(ffn_w_loaded, FFN_LOADS * (layer + 1))
                over_batches(pe, layer, 2, products)

            pipeline(pe, iteration, feed_forward)

        @block.scalar
        def _(act):
            act.wait_ge(consts_set, CONSTS)

            def square(u, j):
                if u is None:
                    return
                act.wait_ge(raw[j], u.g + 1)
                if u.reuses(2):
                    act.wait_ge(summed[j], u.g - 1)
                act.square((sq_q, sq_k)[j][:, u.two, :], psum[:, (RAW_Q, RAW_K)[j], :]).then_inc(squared[j], 1)

            def shift_batch(layer, u):
                if u is None or u.pair:
                    return
                if u.in_layer == 0:
                    act.wait_ge(ffn_added, B * layer + 1)
                else:
                    for part in range(3):
                        act.wait_ge(raw[part], u.g)
                act.copy(xs[0:C // 2, :].unsqueeze(1), sw[0:C // 2, bass.ds(u.batch, 1), :])
                act.copy(xs[C // 2:C, 1:N].unsqueeze(1), sw[C // 2:C, bass.ds(u.batch, 1), 0:N - 1]).then_inc(shifted, 1)

            def copy_q_t(u):
                if u is None:
                    return
                act.wait_ge(turned[0], u.g + 1)
                if u.reuses(2):
                    act.wait_ge(scored[0], u.g - 1)
                    act.wait_ge(scored[1], u.g - 1)
                act.copy(q_t[:, u.two, :], psum[:, TURN_BANKS[0], :]).then_inc(t_ready[0], 1)

            def copy_k_t(u):
                if u is None:
                    return
                act.wait_ge(turned[1], u.g + 1)
                if u.reuses(2):
                    act.wait_ge(scored[0], u.g - 1)
                    act.wait_ge(scored[1], u.g - 1)
                act.copy(k_t[0:DH, u.two, 0, W:], psum[0:DH, TURN_BANKS[1], :])
                act.copy(k_t[DH:P, u.two, 1, W:], psum[DH:P, TURN_BANKS[1], :]).then_inc(t_ready[1], 1)

            def copy_v(u):
                if u is None:
                    return
                act.wait_ge(raw[2], u.g + 1)
                if u.reuses(2):
                    act.wait_ge(v_grouped[(u.four + 2) % 4], 48 * u.fours + (0 if u.four < 2 else 48))
                act.copy(v_rows[:, u.two].rearrange("p t d -> p (t d)"), psum[:, V_ATT, :]).then_inc(v_copied, 1)

            def exps(u, h):
                if u is None:
                    return
                act.wait_ge(biased[h], u.g + 1)
                if u.reuses(2):
                    act.wait_ge(p_turned[h], u.g - 1)
                    act.wait_ge(inverted[h], u.g - 1)
                for t in range(NT):
                    last = act.activation(probs[:, u.two, h, t * GK:(t + 1) * GK],
                                          psum[:, S_A + h, t * GK:(t + 1) * GK], ACT.Exp,
                                          bias=nbias[:, u.two, h, t:t + 1],
                                          scale=rnorm[:, u.four, 2 * t + h:2 * t + h + 1],
                                          accum_out=den[:, u.two, h, t:t + 1])
                last.then_inc(exped[h], 1)

            def copy_probs_t(u, h):
                if u is None:
                    return
                act.wait_ge(p_turned[h], u.g + 1)
                if u.reuses(1):
                    act.wait_ge(attended, u.g + 4)
                act.copy(probs_t[:, h, :], psum[:GK, P_BANKS[h], :]).then_inc(p_t_ready[h], 1)

            def iteration(layer, at):
                shift_batch(layer, at(0))
                copy_probs_t(at(4), 1)
                exps(at(3), 1)
                copy_k_t(at(2))
                square(at(0), 1)
                exps(at(3), 0)
                square(at(0), 0)
                copy_q_t(at(1))
                copy_v(at(0))

            def feed_forward(layer):
                def statistics(at):
                    b = at(0)
                    if b is not None:
                        act.wait_ge(centred, b.n + 1)
                        if b.reuses(2):
                            act.wait_ge(var_ready, b.n - 1)
                        act.square(xsq[:, b.two, :].unsqueeze(1), work[:, bass.ds(b.b, 1), :]).then_inc(f_squared, 1)

                def gates(at):
                    a, b = at(0), at(1)
                    if b is not None:
                        for j, (f0, fn) in enumerate(FB):
                            act.wait_ge(gate_raw, 3 * b.n + j + 1)
                            act.activation(gate[:fn, b.two, j, :], psum[:fn, j, :], ACT.Gelu,
                                           bias=cols[:fn, 6 + j:7 + j]).then_inc(gelu_done, 1)
                    if a is not None:
                        act.wait_ge(scaled, a.n + 1)
                        x = work[:, bass.ds(a.b, 1), :]
                        act.activation(x, x, ACT.Identity, bias=cols[:, 1:2], scale=cols[:, 0:1]).then_inc(ln_done, 1)

                over_batches(act, layer, 0, statistics)
                act.wait_ge(ffn_w_loaded, FFN_LOADS * (layer + 1))
                over_batches(act, layer, 1, gates)

            pipeline(act, iteration, feed_forward)

        @block.vector
        def _(dve):
            for counted in (ffn_added, att_added, projected):
                dve.sem_inc(counted, 1)
            dve.sem_inc(var_copied, 2)
            dve.sem_inc(attended, 4)
            dve.memset(mean_w[:], 1.0 / C).then_inc(consts_set, 1)
            dve.memset(ones[:], 1.0).then_inc(consts_set, 1)
            dve.memset(k_t[:], 0.0).then_inc(consts_set, 1)
            dve.memset(xf[C // 2:C, :, 0:1], 0.0).then_inc(pad_zeroed, 1)
            dve.memset(xs[:], 0.0).then_inc(consts_set, 1)
            dve.wait_ge(consts_loaded, 64)
            dve.tensor_copy(mask[:], sq_q[:, 0, :NT * GK]).then_inc(consts_set, 1)
            dve.tensor_copy(identb[:], ident[:]).then_inc(consts_set, 1)
            dve.wait_ge(consts_set, CONSTS)

            def multiply(u, j):
                if u is None:
                    return
                if u.in_layer == 0:
                    dve.wait_ge(tables_ready, 4 * u.layer + 4)
                dve.wait_ge(squared[j], u.g + 1)
                if u.reuses(2):
                    dve.wait_ge(rotated[j], u.g - 1)
                for i in range(2):
                    last = dve.tensor_tensor(products_of[:, 2 * j + i, u.two, :], psum[:, (RAW_Q, RAW_K)[j], :],
                                             table[:, 2 * j + i, :], ALU.mult)
                last.then_inc(multiplied[j], 1)

            def add_squares(u, j):
                if u is None:
                    return
                dve.wait_ge(squared[j], u.g + 1)
                if u.reuses(2):
                    dve.wait_ge(normed[NEWTON], u.g - 1)
                dve.tensor_reduce(sums[:, u.two, 8 * j:8 * j + 8], (sq_q, sq_k)[j][:, u.two, :]
                                  .rearrange("p (a d) -> p a d", d=DH), AX.X, ALU.add).then_inc(summed[j], 1)

            def invert_norms(u, first, count):
                if u is None:
                    return
                for i in range(first, first + count):
                    x = sums[:, u.two, :]
                    if i == 0:
                        dve.wait_ge(summed[0], u.g + 1)
                        dve.wait_ge(summed[1], u.g + 1)
                        if u.reuses(1):
                            dve.wait_ge(normed[NEWTON], u.g)
                        dve.tensor_scalar(x, x, 1e-24, None, ALU.max).then_inc(normed[0], 1)
                        continue
                    dve.wait_ge(normed[i - 1], u.g + 1)
                    if i == 1 and u.reuses(4):
                        dve.wait_ge(exped[0], u.g - 3)
                        dve.wait_ge(exped[1], u.g - 3)
                        dve.wait_ge(k_scaled, u.g - 3)
                    newton_step(dve, i - 1, rnorm[:, u.four, :], x, ntmp[:]).then_inc(normed[i], 1)

            def row_maxima(u, h):
                if u is None:
                    return
                dve.wait_ge(scored[h], u.g + 1)
                if u.reuses(2):
                    dve.wait_ge(biased[h], u.g - 1)
                dve.tensor_reduce(top[:, u.two, h, :], psum[:, S_A + h, :NT * GK].rearrange("p (t k) -> p t k", t=NT),
                                  AX.X, ALU.max).then_inc(maxed[h], 1)

            def bias(u, h):
                if u is None:
                    return
                dve.wait_ge(maxed[h], u.g + 1)
                dve.wait_ge(normed[NEWTON], u.g + 1)
                if u.reuses(2):
                    dve.wait_ge(exped[h], u.g - 1)
                dve.scalar_tensor_tensor(
                    out=nbias[:, u.two, h, :], in0=top[:, u.two, h, :], scalar=-1.0,
                    in1=rnorm[:, u.four, 0:8].rearrange("p (t h) -> p h t", h=2)[:, h], op0=ALU.mult,
                    op1=ALU.mult).then_inc(biased[h], 1)

            def invert_sums(u, h):
                if u is None:
                    return
                dve.wait_ge(exped[h], u.g + 1)
                if u.reuses(2):
                    dve.wait_ge(weighed[h], u.g - 1)
                dve.reciprocal(rden[:, u.two, h, :], den[:, u.two, h, :]).then_inc(inverted[h], 1)

            def copy_probs_t(u, h):
                if u is None:
                    return
                dve.wait_ge(p_turned[h], u.g + 1)
                if u.reuses(1):
                    dve.wait_ge(attended, u.g + 4)
                dve.tensor_copy(probs_t[:, h, :], psum[:GK, P_BANKS[h], :]).then_inc(p_t_ready[h], 1)

            def copy_attended(u):
                if u is None:
                    return
                dve.wait_ge(attended, u.g + 5)
                if u.reuses(1):
                    dve.wait_ge(projected, u.g + 1)
                dve.tensor_copy(att_t[:], psum[:, V_ATT, :]).then_inc(att_t_ready, 1)

            def add_attention(u):
                if u is None or u.pair != PAIRS - 1:
                    return
                dve.wait_ge(projected, u.g + 2)
                xb = sw[:, bass.ds(u.batch, 1), :]
                dve.tensor_tensor(xb, psum[:, OUT, :].unsqueeze(1), xb, ALU.add).then_inc(att_added, 1)

            def shift_for_norm(layer, u):
                if u is None or u.pair != PAIRS - 1:
                    return
                dve.wait_ge(att_added, u.batches + 2)
                dve.wait_ge(pad_zeroed, layer + 1)
                b = bass.ds(u.batch, 1)
                dve.tensor_copy(xf[0:C // 2, b, :], sw[0:C // 2, b, :])
                dve.tensor_copy(xf[C // 2:C, b, 1:N], sw[C // 2:C, b, 0:N - 1]).then_inc(f_shifted, 1)

            def iteration(layer, at):
                copy_attended(at(4))
                invert_norms(at(1), 8, 1)
                add_squares(at(0), 1)
                invert_norms(at(1), 9, 1)
                row_maxima(at(2), 1)
                invert_sums(at(3), 0)
                invert_norms(at(1), 10, 1)
                multiply(at(0), 1)
                bias(at(2), 1)
                multiply(at(0), 0)
                add_squares(at(0), 0)
                copy_probs_t(at(3), 0)
                invert_norms(at(0), 0, 2)
                add_attention(at(4))
                shift_for_norm(layer, at(4))
                invert_norms(at(0), 2, 1)
                row_maxima(at(2), 0)
                invert_norms(at(0), 3, 2)
                invert_sums(at(2), 1)
                invert_norms(at(0), 5, 1)
                bias(at(2), 0)
                invert_norms(at(0), 6, 2)

            def feed_forward(layer):
                def statistics(at):
                    b = at(0)
                    if b is not None:
                        dve.wait_ge(mean_ready, b.n + 1)
                        x = work[:, bass.ds(b.b, 1), :]
                        dve.tensor_tensor(x, xf[:, bass.ds(b.b, 1), :], psum[:, b.two, :].unsqueeze(1), ALU.subtract) \
                            .then_inc(centred, 1)
                    c = at(2)
                    if c is not None:
                        dve.wait_ge(var_ready, c.n + 1)
                        dve.tensor_scalar(var[:, bass.ds(NT * c.b, NT)], psum[:, 2 + c.two, 0:NT], LN_EPS, None, ALU.add) \
                            .then_inc(var_copied, 1)

                def scale_by_rstd(a):
                    if a is None:
                        return
                    dve.wait_ge(rstd_spread, a.n + 1)
                    x = work[:, bass.ds(a.b, 1), :]
                    dve.tensor_tensor(x, psum[:, SPREAD, :].unsqueeze(1), x, ALU.mult).then_inc(scaled, 1)

                def hidden(at):
                    a, b = at(0), at(1)
                    scale_by_rstd(a)
                    if b is not None:
                        for j, (f0, fn) in enumerate(FB):
                            dve.wait_ge(gelu_done, 3 * b.n + j + 1)
                            dve.wait_ge(hid_raw, 3 * b.n + j + 1)
                            dve.scalar_tensor_tensor(out=hid[:fn, b.two, j, :], in0=psum[:fn, 3 + j, :],
                                                     scalar=cols[:fn, 3 + j:4 + j], in1=gate[:fn, b.two, j, :],
                                                     op0=ALU.add, op1=ALU.mult).then_inc(hid_ready, 1)
                    c = at(2)
                    if c is not None:
                        dve.wait_ge(ffn_raw, c.n + 1)
                        xb = sw[:, bass.ds(c.b, 1), :]
                        dve.scalar_tensor_tensor(out=xb, in0=psum[:, FFN_OUT, :].unsqueeze(1), scalar=cols[:, 2:3], in1=xb,
                                                 op0=ALU.add, op1=ALU.add).then_inc(ffn_added, 1)

                over_batches(dve, layer, 2, statistics)
                dve.wait_ge(var_copied, B * (layer + 1) + 2)
                for i in range(NEWTON):
                    newton_step(dve, i, rstd[:], var[:], ftmp[:]).then_inc(rstd_step, 1)
                    dve.wait_ge(rstd_step, NEWTON * layer + i + 1)
                dve.wait_ge(ffn_w_loaded, FFN_LOADS * (layer + 1))
                over_batches(dve, layer, 2, hidden)
                dve.wait_ge(ffn_added, B * (layer + 1) + 1)
                dve.memset(xf[C // 2:C, :, 0:1], 0.0).then_inc(pad_zeroed, 1)

            pipeline(dve, iteration, feed_forward)

        @block.gpsimd
        def _(pool):
            pool.memset(v_grp[:], 0.0).then_inc(consts_set, 1)
            pool.wait_ge(consts_loaded, 64)

            def rotate(u, j):
                if u is None:
                    return
                pool.wait_ge(multiplied[j], u.g + 1)
                if u.reuses(2):
                    pool.wait_ge(turned[j], u.g - 1)
                a, b, o = (x.rearrange("p (a s d) -> p a s d", s=2, d=DH // 2)
                           for x in (products_of[:, 2 * j, u.two, :], products_of[:, 2 * j + 1, u.two, :],
                                     (q_rot, k_rot)[j][:, u.two, :]))
                for i in range(2):
                    last = pool.tensor_tensor(o[:, :, i, :], a[:, :, i, :], b[:, :, 1 - i, :], ALU.add)
                last.then_inc(rotated[j], 1)

            def scale_k(u):
                if u is None:
                    return
                pool.wait_ge(rotated[1], u.g + 1)
                pool.wait_ge(normed[NEWTON], u.g + 1)
                kr = k_rot[:, u.two, :].rearrange("p (a d) -> p a d", d=DH)
                pool.tensor_tensor(kr, kr, rnorm[:, u.four, 8:16].unsqueeze(2).broadcast_to([P, 8, DH]),
                                   ALU.mult).then_inc(k_scaled, 1)

            def weigh(u, h):
                if u is None:
                    return
                pool.wait_ge(inverted[h], u.g + 1)
                pr = probs[:, u.two, h, :].rearrange("p (t k) -> p t k", t=NT)
                pool.tensor_tensor(pr, pr, rden[:, u.two, h, :].unsqueeze(2).broadcast_to([P, NT, GK]),
                                   ALU.mult).then_inc(weighed[h], 1)

            def iteration(layer, at):
                u = at(0)
                if u is not None and u.in_layer == 0:
                    pool.wait_ge(projected, UNITS * layer + 1)
                    for i in range(4):
                        sc = scales[:, i // 2, bass.ds(layer, 1), :].broadcast_to([P, N // DH, DH])
                        pool.tensor_tensor(table[:, i, :].rearrange("p (a d) -> p a d", d=DH),
                                           base[:, i, :].rearrange("p (a d) -> p a d", d=DH), sc,
                                           ALU.mult).then_inc(tables_ready, 1)
                rotate(at(0), 1)
                rotate(at(0), 0)
                weigh(at(2), 1)
                weigh(at(2), 0)
                scale_k(at(0))

            def feed_forward(layer):
                pool.wait_ge(rstd_step, NEWTON * (layer + 1))

                def spread_rows(at):
                    b = at(0)
                    if b is not None:
                        if b.reuses(2):
                            pool.wait_ge(rstd_spread, b.n - 1)
                        pool.tensor_tensor(rstd_rows[:, b.two, :].rearrange("p (t c) -> p t c", t=NT),
                                           ones[:].unsqueeze(1).broadcast_to([P, NT, P]),
                                           rstd[:, bass.ds(NT * b.b, NT)].unsqueeze(2).broadcast_to([P, NT, P]),
                                           ALU.mult).then_inc(rstd_rows_ready, 1)

                over_batches(pool, layer, 0, spread_rows)

            pipeline(pool, iteration, feed_forward)


def finish(nc, out, x_rows, state, ident, psum):
    with ExitStack() as ctx:
        turned = ctx.enter_context(nc.semaphore("out_turned"))
        added = ctx.enter_context(nc.semaphore("out_added"))
        stored = ctx.enter_context(nc.semaphore("out_stored"))
        out_v = out.rearrange("b (t p) c -> p (b t) c", p=P)
        block = ctx.enter_context(nc.Block())

        @block.tensor
        def _(pe):
            for b in range(B):
                for t in range(NT):
                    last = pe.transpose(psum[:, b, t * P:(t + 1) * P], state[:, b * N + t * P:b * N + (t + 1) * P], ident[:])
                last.then_inc(turned, 1)

        @block.vector
        def _(dve):
            for b in range(B):
                dve.wait_ge(turned, b + 1)
                xb = x_rows[:, b * NT:(b + 1) * NT, :].rearrange("p t c -> p (t c)")
                dve.tensor_tensor(xb, psum[:, b, :], xb, ALU.add).then_inc(added, 1)

        @block.sync
        def _(sp):
            for b in range(B):
                sp.wait_ge(added, b + 1)
                sp.dma_start(out_v[:, b * NT:(b + 1) * NT, :], x_rows[:, b * NT:(b + 1) * NT, :]).then_inc(stored, 16)
            sp.wait_ge(stored, 16 * B)


def build(nc, x, wk, bk, wq, bq, wv, bv, wp, bp, w_qkv, q_scale, k_scale, w_o, w_1, w_2, columns, rotary,
          window_mask, causal_masks, ident32, out):
    with ExitStack() as ctx:
        x_rows = ctx.enter_context(nc.sbuf_tensor("x_rows", [P, RT, C], F32))
        state = ctx.enter_context(nc.sbuf_tensor("state", [P, ROWS], F32))
        ident = ctx.enter_context(nc.sbuf_tensor("ident", [P, P], F32))
        psum = ctx.enter_context(nc.psum_tensor("psum", [P, 8, 512], F32))
        layernorm_to_state(nc, x, ident32, x_rows, state, ident, psum)
        causal_attention(nc, wk, bk, wq, bq, wv, bv, wp, bp, causal_masks, x_rows, state, ident, psum)
        layers(nc, w_qkv, q_scale, k_scale, w_o, w_1, w_2, columns, rotary, window_mask, state, ident, psum)
        finish(nc, out, x_rows, state, ident, psum)


def shape_constants():
    import numpy as np
    f = np.float32
    half = np.arange(0, DH, 2, dtype=f)
    inv_freq = (f(1.0) / f(10000.0) ** (half / f(DH))).astype(f)
    t = np.arange(N, dtype=f)
    freqs = (t[:, None] * inv_freq[None, :]).astype(f)
    base = ((half + f(0.4 * DH)) / f(1.4 * DH)).astype(f)
    power = ((t - f(N // 2)) / f(W // 2)).astype(f)
    scale = (base[None, :] ** power[:, None]).astype(f)
    cos, sin = np.cos(freqs), np.sin(freqs)
    inv = (f(1.0) / scale).astype(f)

    def both(a, b):
        one = np.concatenate([a, b], 1).reshape(N // P, P, 1, DH)
        return np.repeat(one, 2, 2).transpose(1, 0, 2, 3).reshape(P, N)

    rotary = np.stack([both(8 * cos * scale, 8 * cos * scale), both(8 * sin * scale, -8 * sin * scale),
                       both(cos * inv, cos * inv), both(sin * inv, -sin * inv)]).astype(f)
    r, c = np.arange(GQ)[:, None], np.arange(GK)[None, :]
    band = (c >= r) & (c <= r + W)
    mask = np.zeros((2, GQ, N // P, GK), f)
    mask[:] = np.where(band, 0.0, -1e20)[None, :, None, :]
    mask[0, :, 0, :] = np.where(band & (c >= W), 0.0, -1e20)
    rows = np.where(np.tril(np.ones((P, P), bool)), 0.0, -1e30)
    causal = np.stack([rows, rows.T], 1)
    return rotary, mask.reshape(P, -1), causal.astype(f)


_NAMES = ["x", "Wk", "bk", "Wq", "bq", "Wv", "bv", "Wp", "bp"]


def inputs_for(inputs):
    import numpy as np
    a = {n: np.asarray(inputs["L0_attn_" + n]) for n in _NAMES}
    f = {n[7:]: np.asarray(v) for n, v in inputs.items() if n.startswith("L0_ffn_")}
    columns = np.zeros((DEPTH, P, 9), np.float32)
    columns[:, :, 0], columns[:, :, 1], columns[:, :, 2] = f["ln_g"], f["ln_b"], f["b2"]
    for j, (f0, fn) in enumerate(FB):
        columns[:, :fn, 3 + j] = f["b1"][:, f0:f0 + fn]
        columns[:, :fn, 6 + j] = f["b1"][:, FI + f0:FI + f0 + fn]
    rotary, mask, causal = shape_constants()
    return {"x": a["x"], "wk": a["Wk"], "bk": a["bk"], "wq": a["Wq"], "bq": a["bq"], "wv": a["Wv"], "bv": a["bv"],
            "wp": a["Wp"], "bp": a["bp"], "w_qkv": f["Wqkv"], "q_scale": f["q_scale"], "k_scale": f["k_scale"],
            "w_o": f["Wo"], "w_1": f["W1"], "w_2": f["W2"], "columns": columns, "rotary": rotary,
            "window_mask": mask, "causal_masks": causal, "ident32": np.eye(P, dtype=np.float32)}


def kernel(**inputs):
    import numpy as np
    import concourse.bacc as bacc
    from concourse.bass_utils import run_bass_kernel_spmd

    arrays = {n: np.ascontiguousarray(v) for n, v in inputs_for(inputs).items()}
    nc = bacc.Bacc("TRN2", target_bir_lowering=False, num_devices=1)
    args = [nc.dram_tensor(n, v.shape, mybir.dt.from_np(v.dtype), kind="ExternalInput").ap() for n, v in arrays.items()]
    out = nc.dram_tensor("out", (B, N, C), F32, kind="ExternalOutput").ap()
    build(nc, *args, out)
    return run_bass_kernel_spmd(nc, [arrays], core_ids=[0]).results[0]["out"]
```
